# Optimizing a Trainium2 kernel written in Bass

```python
import numpy as np
import jax
import jax.numpy as jnp

def _softmax(x, axis=-1):
    return jax.nn.softmax(x, axis=axis)

def _gelu(x):
    return jax.nn.gelu(x, approximate=True)

def _silu(x):
    return jax.nn.silu(x)

def _sigmoid(x):
    return jax.nn.sigmoid(x)

def _layernorm(x, axis=-1, eps=1e-05):
    m = jnp.mean(x, axis=axis, keepdims=True)
    v = jnp.var(x, axis=axis, keepdims=True)
    return (x - m) / jnp.sqrt(v + eps)

def _scatter_add(tgt, idx, src, axis=0):
    return tgt.at[idx].add(src)

def _segment_sum(src, seg, n):
    return jax.ops.segment_sum(src, seg, n)
kernel_name = 'mk_conv_seq_d4_conv_nhwc256_r4_f5834a'

def setup_inputs(seed: int=0):
    np.random.seed(seed)
    _w = jnp.asarray

    def _rec_inputs():
        import jax
        import jax.numpy as jnp
        _gk = jax.random.key(seed)
        x = 0.0003368 + 1 * jax.random.normal(jax.random.fold_in(_gk, 1), (32, 56, 56, 64), jnp.float32)
        return x
    x = _rec_inputs()

    def _L0_conv_setup():
        import jax, jax.numpy as jnp
        import numpy as np
        key = jax.random.key(seed)
        inputs = jax.random.normal(key, (32, 56, 56, 64), dtype=jnp.float32)
        return {'inputs': inputs}
    _L0_conv_all = _L0_conv_setup()
    _L0_conv_in = {k: v for k, v in _L0_conv_all.items() if k in ()}
    del _L0_conv_all

    def _L1_conv_setup():
        import jax, jax.numpy as jnp
        import numpy as np
        from jax import lax
        EPS = 0.001
        DN = ('NHWC', 'HWIO', 'NHWC')

        def _bn(x, gamma, beta, mean, var):
            inv = gamma * lax.rsqrt(var + EPS)
            return x * inv + (beta - mean * inv)
        key = jax.random.key(seed)
        ks = jax.random.split(key, 5)
        B, H, W, C = (32, 56, 56, 64)
        G, CG = (32, 4)
        CM = G * CG
        x = jax.random.normal(ks[0], (B, H, W, C), jnp.float32)
        w1 = jax.random.normal(ks[1], (1, 1, C, CM), jnp.float32) * 0.05
        b1 = jnp.zeros((CM,), jnp.float32)
        g1 = jnp.ones((CM,), jnp.float32)
        be1 = jnp.zeros((CM,), jnp.float32)
        m1 = jnp.zeros((CM,), jnp.float32)
        v1 = jnp.ones((CM,), jnp.float32)
        w2 = jax.random.normal(ks[2], (3, 3, CG, CM), jnp.float32) * 0.1
        b2 = jnp.zeros((CM,), jnp.float32)
        g2 = jnp.ones((CM,), jnp.float32)
        be2 = jnp.zeros((CM,), jnp.float32)
        m2 = jnp.zeros((CM,), jnp.float32)
        v2 = jnp.ones((CM,), jnp.float32)
        w3 = jax.random.normal(ks[3], (1, 1, CM, C), jnp.float32) * 0.05
        b3 = jnp.zeros((C,), jnp.float32)
        return dict(x=x, w1=w1, b1=b1, g1=g1, be1=be1, m1=m1, v1=v1, w2=w2, b2=b2, g2=g2, be2=be2, m2=m2, v2=v2, w3=w3, b3=b3)
    _L1_conv_all = _L1_conv_setup()
    _L1_conv_in = {k: v for k, v in _L1_conv_all.items() if k in ('w1', 'b1', 'g1', 'be1', 'm1', 'v1', 'w2', 'b2', 'g2', 'be2', 'm2', 'v2', 'w3', 'b3')}
    del _L1_conv_all

    def _L2_conv_setup():
        import jax, jax.numpy as jnp
        import numpy as np
        DIM = 64
        HEADS = 8
        WS = 8
        N = WS * WS
        NF = 2 * (N // 2 + 1)
        HD = DIM // HEADS
        SCALE = HD ** (-0.5)
        EPS = 1e-05

        def _rel_pos_index():
            ch = np.arange(WS)
            coords = np.stack(np.meshgrid(ch, ch, indexing='ij'))
            cf = coords.reshape(2, -1)
            rel = cf[:, :, None] - cf[:, None, :]
            rel = rel.transpose(1, 2, 0).astype(np.int64)
            rel[..., 0] += WS - 1
            rel[..., 1] += WS - 1
            rel[..., 0] *= 2 * WS - 1
            return jnp.asarray(rel.sum(-1))
        REL_IDX = _rel_pos_index()

        def _ln(x, w, b):
            m = jnp.mean(x, -1, keepdims=True)
            v = jnp.mean((x - m) ** 2, -1, keepdims=True)
            return (x - m) * jax.lax.rsqrt(v + EPS) * w + b

        def _attn_scores(t, qkv_w, qkv_b):
            Bw, Nt, C = t.shape
            qkv = (t @ qkv_w.T + qkv_b).reshape(Bw, Nt, 3, HEADS, HD)
            q, k, v = jnp.moveaxis(qkv, 2, 0)
            q = q.transpose(0, 2, 1, 3)
            k = k.transpose(0, 2, 1, 3)
            v = v.transpose(0, 2, 1, 3)
            a = jnp.einsum('bhnd,bhmd->bhnm', q, k) * SCALE
            return (a, v)
        key = jax.random.key(seed)
        ks = jax.random.split(key, 16)
        B, H, W, C = (2, 64, 64, DIM)
        p = 0.02
        return {'x': jax.random.normal(ks[0], (B, H, W, C), jnp.float32), 'mask_matrix': jnp.zeros((H // WS * (W // WS), N, N), jnp.float32), 'norm1_w': jnp.ones((C,), jnp.float32), 'norm1_b': jnp.zeros((C,), jnp.float32), 'qkv_w': jax.random.normal(ks[1], (3 * C, C), jnp.float32) * p, 'qkv_b': jnp.zeros((3 * C,), jnp.float32), 'rpb_table': jax.random.normal(ks[2], ((2 * WS - 1) ** 2, HEADS), jnp.float32) * p, 'proj_w': jax.random.normal(ks[3], (C, C), jnp.float32) * p, 'proj_b': jnp.zeros((C,), jnp.float32), 'norm2_w': jnp.ones((C,), jnp.float32), 'norm2_b': jnp.zeros((C,), jnp.float32), 'fc1_w': jax.random.normal(ks[4], (4 * C, C), jnp.float32) * p, 'fc1_b': jnp.zeros((4 * C,), jnp.float32), 'fc2_w': jax.random.normal(ks[5], (C, 4 * C), jnp.float32) * p, 'fc2_b': jnp.zeros((C,), jnp.float32)}
    _L2_conv_all = _L2_conv_setup()
    _L2_conv_in = {k: v for k, v in _L2_conv_all.items() if k in ('mask_matrix', 'norm1_w', 'norm1_b', 'qkv_w', 'qkv_b', 'rpb_table', 'proj_w', 'proj_b', 'norm2_w', 'norm2_b', 'fc1_w', 'fc1_b', 'fc2_w', 'fc2_b')}
    del _L2_conv_all

    def _L3_conv_setup():
        import jax, jax.numpy as jnp
        import numpy as np
        C = 64
        G = 16
        GC = C // G
        K = 3
        PAD = 1
        DIL = 1
        OFFSET_SCALE = 1.0
        MLP_HIDDEN = 256
        EPS = 1e-06

        def ln(x, g, b):
            mu = jnp.mean(x, axis=-1, keepdims=True)
            var = jnp.mean((x - mu) ** 2, axis=-1, keepdims=True)
            return (x - mu) * jax.lax.rsqrt(var + EPS) * g + b

        def dcnv3(x, dw_w, dw_b, dwln_g, dwln_b, off_w, off_b, mask_w, mask_b, inproj_w, inproj_b, outproj_w, outproj_b):
            N, H, W, _ = x.shape
            P = K * K
            x_proj = x @ inproj_w + inproj_b
            x1 = jax.lax.conv_general_dilated(x, dw_w, (1, 1), [(PAD, PAD), (PAD, PAD)], dimension_numbers=('NHWC', 'HWIO', 'NHWC'), feature_group_count=C) + dw_b
            x1 = jax.nn.gelu(ln(x1, dwln_g, dwln_b), approximate=False)
            offset = (x1 @ off_w + off_b).reshape(N, H, W, G, P, 2)
            mask = jax.nn.softmax((x1 @ mask_w + mask_b).reshape(N, H, W, G, P), axis=-1)
            xp = jnp.pad(x_proj, ((0, 0), (PAD, PAD), (PAD, PAD), (0, 0)))
            Hin, Win = (H + 2 * PAD, W + 2 * PAD)
            base = DIL * (K - 1) // 2 + 0.5
            ref_x = (base + jnp.arange(W, dtype=x.dtype)) / Win
            ref_y = (base + jnp.arange(H, dtype=x.dtype)) / Hin
            offs = jnp.arange(K, dtype=x.dtype) * DIL - DIL * (K - 1) // 2
            gx, gy = jnp.meshgrid(offs / Win, offs / Hin, indexing='ij')
            grid_x = gx.reshape(-1)
            grid_y = gy.reshape(-1)
            loc_x = ref_x[None, None, :, None, None] + grid_x * OFFSET_SCALE + offset[..., 0] * (OFFSET_SCALE / Win)
            loc_y = ref_y[None, :, None, None, None] + grid_y * OFFSET_SCALE + offset[..., 1] * (OFFSET_SCALE / Hin)
            px = loc_x * Win - 0.5
            py = loc_y * Hin - 0.5
            img = xp.reshape(N, Hin, Win, G, GC).transpose(0, 3, 1, 2, 4)
            x0 = jnp.floor(px)
            y0 = jnp.floor(py)
            lx = px - x0
            ly = py - y0
            x0 = x0.astype(jnp.int32)
            y0 = y0.astype(jnp.int32)
            n_ix = jnp.arange(N)[:, None, None, None, None]
            g_ix = jnp.arange(G)[None, None, None, :, None]

            def gather(yi, xi):
                valid = ((yi >= 0) & (yi < Hin) & (xi >= 0) & (xi < Win)).astype(xp.dtype)
                yc = jnp.clip(yi, 0, Hin - 1)
                xc = jnp.clip(xi, 0, Win - 1)
                return img[n_ix, g_ix, yc, xc] * valid[..., None]
            val = gather(y0, x0) * ((1 - ly) * (1 - lx))[..., None] + gather(y0, x0 + 1) * ((1 - ly) * lx)[..., None] + gather(y0 + 1, x0) * (ly * (1 - lx))[..., None] + gather(y0 + 1, x0 + 1) * (ly * lx)[..., None]
            out = jnp.einsum('nhwgpc,nhwgp->nhwgc', val, mask).reshape(N, H, W, C)
            return out @ outproj_w + outproj_b
        key = jax.random.key(seed)
        ks = jax.random.split(key, 10)
        N, H, W = (4, 56, 56)
        s = 0.02
        P = K * K
        return {'x': jax.random.normal(ks[0], (N, H, W, C), jnp.float32), 'ln1_g': jnp.ones((C,), jnp.float32), 'ln1_b': jnp.zeros((C,), jnp.float32), 'dw_w': jax.random.normal(ks[1], (K, K, 1, C), jnp.float32) * s, 'dw_b': jnp.zeros((C,), jnp.float32), 'dwln_g': jnp.ones((C,), jnp.float32), 'dwln_b': jnp.zeros((C,), jnp.float32), 'off_w': jax.random.normal(ks[2], (C, G * P * 2), jnp.float32) * s, 'off_b': jnp.zeros((G * P * 2,), jnp.float32), 'mask_w': jax.random.normal(ks[3], (C, G * P), jnp.float32) * s, 'mask_b': jnp.zeros((G * P,), jnp.float32), 'inproj_w': jax.random.normal(ks[4], (C, C), jnp.float32) * s, 'inproj_b': jnp.zeros((C,), jnp.float32), 'outproj_w': jax.random.normal(ks[5], (C, C), jnp.float32) * s, 'outproj_b': jnp.zeros((C,), jnp.float32), 'ln2_g': jnp.ones((C,), jnp.float32), 'ln2_b': jnp.zeros((C,), jnp.float32), 'fc1_w': jax.random.normal(ks[6], (C, MLP_HIDDEN), jnp.float32) * s, 'fc1_b': jnp.zeros((MLP_HIDDEN,), jnp.float32), 'fc2_w': jax.random.normal(ks[7], (MLP_HIDDEN, C), jnp.float32) * s, 'fc2_b': jnp.zeros((C,), jnp.float32)}
    _L3_conv_all = _L3_conv_setup()
    _L3_conv_in = {k: v for k, v in _L3_conv_all.items() if k in ('ln1_g', 'ln1_b', 'dw_w', 'dw_b', 'dwln_g', 'dwln_b', 'off_w', 'off_b', 'mask_w', 'mask_b', 'inproj_w', 'inproj_b', 'outproj_w', 'outproj_b', 'ln2_g', 'ln2_b', 'fc1_w', 'fc1_b', 'fc2_w', 'fc2_b')}
    del _L3_conv_all
    return {'x': x, 'L1_conv_w1': _L1_conv_in['w1'], 'L1_conv_b1': _L1_conv_in['b1'], 'L1_conv_g1': _L1_conv_in['g1'], 'L1_conv_be1': _L1_conv_in['be1'], 'L1_conv_m1': _L1_conv_in['m1'], 'L1_conv_v1': _L1_conv_in['v1'], 'L1_conv_w2': _L1_conv_in['w2'], 'L1_conv_b2': _L1_conv_in['b2'], 'L1_conv_g2': _L1_conv_in['g2'], 'L1_conv_be2': _L1_conv_in['be2'], 'L1_conv_m2': _L1_conv_in['m2'], 'L1_conv_v2': _L1_conv_in['v2'], 'L1_conv_w3': _L1_conv_in['w3'], 'L1_conv_b3': _L1_conv_in['b3'], 'L2_conv_mask_matrix': _L2_conv_in['mask_matrix'], 'L2_conv_norm1_w': _L2_conv_in['norm1_w'], 'L2_conv_norm1_b': _L2_conv_in['norm1_b'], 'L2_conv_qkv_w': _L2_conv_in['qkv_w'], 'L2_conv_qkv_b': _L2_conv_in['qkv_b'], 'L2_conv_rpb_table': _L2_conv_in['rpb_table'], 'L2_conv_proj_w': _L2_conv_in['proj_w'], 'L2_conv_proj_b': _L2_conv_in['proj_b'], 'L2_conv_norm2_w': _L2_conv_in['norm2_w'], 'L2_conv_norm2_b': _L2_conv_in['norm2_b'], 'L2_conv_fc1_w': _L2_conv_in['fc1_w'], 'L2_conv_fc1_b': _L2_conv_in['fc1_b'], 'L2_conv_fc2_w': _L2_conv_in['fc2_w'], 'L2_conv_fc2_b': _L2_conv_in['fc2_b'], 'L3_conv_ln1_g': _L3_conv_in['ln1_g'], 'L3_conv_ln1_b': _L3_conv_in['ln1_b'], 'L3_conv_dw_w': _L3_conv_in['dw_w'], 'L3_conv_dw_b': _L3_conv_in['dw_b'], 'L3_conv_dwln_g': _L3_conv_in['dwln_g'], 'L3_conv_dwln_b': _L3_conv_in['dwln_b'], 'L3_conv_off_w': _L3_conv_in['off_w'], 'L3_conv_off_b': _L3_conv_in['off_b'], 'L3_conv_mask_w': _L3_conv_in['mask_w'], 'L3_conv_mask_b': _L3_conv_in['mask_b'], 'L3_conv_inproj_w': _L3_conv_in['inproj_w'], 'L3_conv_inproj_b': _L3_conv_in['inproj_b'], 'L3_conv_outproj_w': _L3_conv_in['outproj_w'], 'L3_conv_outproj_b': _L3_conv_in['outproj_b'], 'L3_conv_ln2_g': _L3_conv_in['ln2_g'], 'L3_conv_ln2_b': _L3_conv_in['ln2_b'], 'L3_conv_fc1_w': _L3_conv_in['fc1_w'], 'L3_conv_fc1_b': _L3_conv_in['fc1_b'], 'L3_conv_fc2_w': _L3_conv_in['fc2_w'], 'L3_conv_fc2_b': _L3_conv_in['fc2_b']}

def reference(x, L1_conv_w1, L1_conv_b1, L1_conv_g1, L1_conv_be1, L1_conv_m1, L1_conv_v1, L1_conv_w2, L1_conv_b2, L1_conv_g2, L1_conv_be2, L1_conv_m2, L1_conv_v2, L1_conv_w3, L1_conv_b3, L2_conv_mask_matrix, L2_conv_norm1_w, L2_conv_norm1_b, L2_conv_qkv_w, L2_conv_qkv_b, L2_conv_rpb_table, L2_conv_proj_w, L2_conv_proj_b, L2_conv_norm2_w, L2_conv_norm2_b, L2_conv_fc1_w, L2_conv_fc1_b, L2_conv_fc2_w, L2_conv_fc2_b, L3_conv_ln1_g, L3_conv_ln1_b, L3_conv_dw_w, L3_conv_dw_b, L3_conv_dwln_g, L3_conv_dwln_b, L3_conv_off_w, L3_conv_off_b, L3_conv_mask_w, L3_conv_mask_b, L3_conv_inproj_w, L3_conv_inproj_b, L3_conv_outproj_w, L3_conv_outproj_b, L3_conv_ln2_g, L3_conv_ln2_b, L3_conv_fc1_w, L3_conv_fc1_b, L3_conv_fc2_w, L3_conv_fc2_b):
    import jax
    import jax.numpy as jnp

    def _L0_conv_ref(inputs):
        import jax, jax.numpy as jnp
        import numpy as np
        b, h, w, c = inputs.shape
        x1 = inputs.reshape(b, h * w, c)
        dots = jnp.einsum('bdi,bdj->bij', x1, x1) * c ** (-0.5)
        attn = jax.nn.softmax(dots, axis=-1)
        scale = jnp.einsum('bij,bdj->bdi', attn, x1)
        return scale.reshape(b, h, w, c) + inputs

    def _L1_conv_ref(x, w1, b1, g1, be1, m1, v1, w2, b2, g2, be2, m2, v2, w3, b3):
        import jax, jax.numpy as jnp
        import numpy as np
        from jax import lax
        EPS = 0.001
        DN = ('NHWC', 'HWIO', 'NHWC')

        def _bn(x, gamma, beta, mean, var):
            inv = gamma * lax.rsqrt(var + EPS)
            return x * inv + (beta - mean * inv)
        h = lax.conv_general_dilated(x, w1, (1, 1), 'SAME', dimension_numbers=DN) + b1
        h = jax.nn.relu(_bn(h, g1, be1, m1, v1))
        h = lax.conv_general_dilated(h, w2, (1, 1), 'SAME', dimension_numbers=DN, feature_group_count=32) + b2
        h = jax.nn.relu(_bn(h, g2, be2, m2, v2))
        out = lax.conv_general_dilated(h, w3, (1, 1), 'SAME', dimension_numbers=DN) + b3
        return jax.nn.relu(out + x)

    def _L2_conv_ref(x, mask_matrix, norm1_w, norm1_b, qkv_w, qkv_b, rpb_table, proj_w, proj_b, norm2_w, norm2_b, fc1_w, fc1_b, fc2_w, fc2_b):
        import jax, jax.numpy as jnp
        import numpy as np
        DIM = 64
        HEADS = 8
        WS = 8
        N = WS * WS
        NF = 2 * (N // 2 + 1)
        HD = DIM // HEADS
        SCALE = HD ** (-0.5)
        EPS = 1e-05

        def _rel_pos_index():
            ch = np.arange(WS)
            coords = np.stack(np.meshgrid(ch, ch, indexing='ij'))
            cf = coords.reshape(2, -1)
            rel = cf[:, :, None] - cf[:, None, :]
            rel = rel.transpose(1, 2, 0).astype(np.int64)
            rel[..., 0] += WS - 1
            rel[..., 1] += WS - 1
            rel[..., 0] *= 2 * WS - 1
            return jnp.asarray(rel.sum(-1))
        REL_IDX = _rel_pos_index()

        def _ln(x, w, b):
            m = jnp.mean(x, -1, keepdims=True)
            v = jnp.mean((x - m) ** 2, -1, keepdims=True)
            return (x - m) * jax.lax.rsqrt(v + EPS) * w + b

        def _attn_scores(t, qkv_w, qkv_b):
            Bw, Nt, C = t.shape
            qkv = (t @ qkv_w.T + qkv_b).reshape(Bw, Nt, 3, HEADS, HD)
            q, k, v = jnp.moveaxis(qkv, 2, 0)
            q = q.transpose(0, 2, 1, 3)
            k = k.transpose(0, 2, 1, 3)
            v = v.transpose(0, 2, 1, 3)
            a = jnp.einsum('bhnd,bhmd->bhnm', q, k) * SCALE
            return (a, v)
        B, H, W, C = x.shape
        shortcut = x
        x = _ln(x, norm1_w, norm1_b)
        xw = x.reshape(B, H // WS, WS, W // WS, WS, C).transpose(0, 1, 3, 2, 4, 5).reshape(-1, N, C)
        Bw = xw.shape[0]
        a, v = _attn_scores(xw, qkv_w, qkv_b)
        bias = rpb_table[REL_IDX.reshape(-1)].reshape(N, N, HEADS).transpose(2, 0, 1)
        a = jax.nn.softmax(a + bias[None], axis=-1)
        out = jnp.einsum('bhnm,bhmd->bhnd', a, v).transpose(0, 2, 1, 3).reshape(Bw, N, C)
        xf = jnp.fft.rfft(xw, axis=-2, norm='ortho')
        xf = jnp.concatenate([xf.real, xf.imag], axis=-2)
        af, vf = _attn_scores(xf, qkv_w, qkv_b)
        af = jax.nn.softmax(af, axis=-1)
        outf = jnp.einsum('bhnm,bhmd->bhnd', af, vf).transpose(0, 2, 1, 3).reshape(Bw, NF, C)
        cf = outf[:, :NF // 2] + 1j * outf[:, NF // 2:]
        xr = jnp.fft.irfft(cf, n=N, axis=-2, norm='ortho')
        xa = (out + xr) @ proj_w.T + proj_b
        x = xa.reshape(B, H // WS, W // WS, WS, WS, C).transpose(0, 1, 3, 2, 4, 5).reshape(B, H, W, C)
        x = shortcut + x
        h = _ln(x, norm2_w, norm2_b)
        h = jax.nn.gelu(h @ fc1_w.T + fc1_b, approximate=False)
        x = x + (h @ fc2_w.T + fc2_b)
        return x

    def _L3_conv_ref(x, ln1_g, ln1_b, dw_w, dw_b, dwln_g, dwln_b, off_w, off_b, mask_w, mask_b, inproj_w, inproj_b, outproj_w, outproj_b, ln2_g, ln2_b, fc1_w, fc1_b, fc2_w, fc2_b):
        import jax, jax.numpy as jnp
        import numpy as np
        C = 64
        G = 16
        GC = C // G
        K = 3
        PAD = 1
        DIL = 1
        OFFSET_SCALE = 1.0
        MLP_HIDDEN = 256
        EPS = 1e-06

        def ln(x, g, b):
            mu = jnp.mean(x, axis=-1, keepdims=True)
            var = jnp.mean((x - mu) ** 2, axis=-1, keepdims=True)
            return (x - mu) * jax.lax.rsqrt(var + EPS) * g + b

        def dcnv3(x, dw_w, dw_b, dwln_g, dwln_b, off_w, off_b, mask_w, mask_b, inproj_w, inproj_b, outproj_w, outproj_b):
            N, H, W, _ = x.shape
            P = K * K
            x_proj = x @ inproj_w + inproj_b
            x1 = jax.lax.conv_general_dilated(x, dw_w, (1, 1), [(PAD, PAD), (PAD, PAD)], dimension_numbers=('NHWC', 'HWIO', 'NHWC'), feature_group_count=C) + dw_b
            x1 = jax.nn.gelu(ln(x1, dwln_g, dwln_b), approximate=False)
            offset = (x1 @ off_w + off_b).reshape(N, H, W, G, P, 2)
            mask = jax.nn.softmax((x1 @ mask_w + mask_b).reshape(N, H, W, G, P), axis=-1)
            xp = jnp.pad(x_proj, ((0, 0), (PAD, PAD), (PAD, PAD), (0, 0)))
            Hin, Win = (H + 2 * PAD, W + 2 * PAD)
            base = DIL * (K - 1) // 2 + 0.5
            ref_x = (base + jnp.arange(W, dtype=x.dtype)) / Win
            ref_y = (base + jnp.arange(H, dtype=x.dtype)) / Hin
            offs = jnp.arange(K, dtype=x.dtype) * DIL - DIL * (K - 1) // 2
            gx, gy = jnp.meshgrid(offs / Win, offs / Hin, indexing='ij')
            grid_x = gx.reshape(-1)
            grid_y = gy.reshape(-1)
            loc_x = ref_x[None, None, :, None, None] + grid_x * OFFSET_SCALE + offset[..., 0] * (OFFSET_SCALE / Win)
            loc_y = ref_y[None, :, None, None, None] + grid_y * OFFSET_SCALE + offset[..., 1] * (OFFSET_SCALE / Hin)
            px = loc_x * Win - 0.5
            py = loc_y * Hin - 0.5
            img = xp.reshape(N, Hin, Win, G, GC).transpose(0, 3, 1, 2, 4)
            x0 = jnp.floor(px)
            y0 = jnp.floor(py)
            lx = px - x0
            ly = py - y0
            x0 = x0.astype(jnp.int32)
            y0 = y0.astype(jnp.int32)
            n_ix = jnp.arange(N)[:, None, None, None, None]
            g_ix = jnp.arange(G)[None, None, None, :, None]

            def gather(yi, xi):
                valid = ((yi >= 0) & (yi < Hin) & (xi >= 0) & (xi < Win)).astype(xp.dtype)
                yc = jnp.clip(yi, 0, Hin - 1)
                xc = jnp.clip(xi, 0, Win - 1)
                return img[n_ix, g_ix, yc, xc] * valid[..., None]
            val = gather(y0, x0) * ((1 - ly) * (1 - lx))[..., None] + gather(y0, x0 + 1) * ((1 - ly) * lx)[..., None] + gather(y0 + 1, x0) * (ly * (1 - lx))[..., None] + gather(y0 + 1, x0 + 1) * (ly * lx)[..., None]
            out = jnp.einsum('nhwgpc,nhwgp->nhwgc', val, mask).reshape(N, H, W, C)
            return out @ outproj_w + outproj_b
        x = x + dcnv3(ln(x, ln1_g, ln1_b), dw_w, dw_b, dwln_g, dwln_b, off_w, off_b, mask_w, mask_b, inproj_w, inproj_b, outproj_w, outproj_b)
        h = ln(x, ln2_g, ln2_b)
        x = x + (jax.nn.gelu(h @ fc1_w + fc1_b, approximate=False) @ fc2_w + fc2_b)
        return x

    def _gn(v, G=32, eps=1e-05):
        B_, H_, W_, C_ = v.shape
        g = v.reshape(B_, H_, W_, G, C_ // G)
        m = jnp.mean(g, axis=(1, 2, 4), keepdims=True)
        s = jnp.var(g, axis=(1, 2, 4), keepdims=True)
        return ((g - m) / jnp.sqrt(s + eps)).reshape(v.shape)

    def _ln_c(v, eps=1e-06):
        m = jnp.mean(v, axis=-1, keepdims=True)
        s = jnp.var(v, axis=-1, keepdims=True)
        return (v - m) / jnp.sqrt(s + eps)

    def _ln_t(v, eps=1e-05):
        m = jnp.mean(v, axis=-1, keepdims=True)
        s = jnp.var(v, axis=-1, keepdims=True)
        return (v - m) / jnp.sqrt(s + eps)

    def _to_tokens(v):
        B_, H_, W_, C_ = v.shape
        return v.reshape(B_, H_ * W_, C_)

    def _from_tokens(t, like):
        return t.reshape(like.shape)
    x = _L0_conv_ref(x)
    x = _L1_conv_ref(x, L1_conv_w1, L1_conv_b1, L1_conv_g1, L1_conv_be1, L1_conv_m1, L1_conv_v1, L1_conv_w2, L1_conv_b2, L1_conv_g2, L1_conv_be2, L1_conv_m2, L1_conv_v2, L1_conv_w3, L1_conv_b3)
    x = _L2_conv_ref(x, L2_conv_mask_matrix, L2_conv_norm1_w, L2_conv_norm1_b, L2_conv_qkv_w, L2_conv_qkv_b, L2_conv_rpb_table, L2_conv_proj_w, L2_conv_proj_b, L2_conv_norm2_w, L2_conv_norm2_b, L2_conv_fc1_w, L2_conv_fc1_b, L2_conv_fc2_w, L2_conv_fc2_b)
    x = _L3_conv_ref(x, L3_conv_ln1_g, L3_conv_ln1_b, L3_conv_dw_w, L3_conv_dw_b, L3_conv_dwln_g, L3_conv_dwln_b, L3_conv_off_w, L3_conv_off_b, L3_conv_mask_w, L3_conv_mask_b, L3_conv_inproj_w, L3_conv_inproj_b, L3_conv_outproj_w, L3_conv_outproj_b, L3_conv_ln2_g, L3_conv_ln2_b, L3_conv_fc1_w, L3_conv_fc1_b, L3_conv_fc2_w, L3_conv_fc2_b)
    return x

_drawn_inputs = setup_inputs


def setup_inputs(seed=0):
    import zlib

    import numpy as np

    out = dict(_drawn_inputs(seed))
    spreads = {'L1_conv_b1': (0.0, 0.8),
     'L1_conv_g1': (1.0, 0.6),
     'L1_conv_be1': (0.0, 0.8),
     'L1_conv_m1': (0.0, 0.8),
     'L1_conv_v1': (1.0, 0.6),
     'L1_conv_b2': (0.0, 0.406),
     'L1_conv_g2': (1.0, 0.6),
     'L1_conv_be2': (0.0, 0.389),
     'L1_conv_m2': (0.0, 0.436),
     'L1_conv_v2': (1.0, 0.6),
     'L1_conv_b3': (0.0, 0.1),
     'L2_conv_mask_matrix': (0.0, 0.1),
     'L2_conv_norm1_w': (1.0, 0.6),
     'L2_conv_norm1_b': (0.0, 0.8),
     'L2_conv_qkv_b': (0.0, 0.387),
     'L2_conv_proj_b': (0.0, 0.1),
     'L2_conv_norm2_w': (1.0, 0.6),
     'L2_conv_norm2_b': (0.0, 2.0),
     'L2_conv_fc1_b': (0.0, 0.688),
     'L2_conv_fc2_b': (0.0, 0.1),
     'L3_conv_ln1_g': (1.0, 0.6),
     'L3_conv_ln1_b': (0.0, 0.8),
     'L3_conv_dw_b': (0.0, 0.8),
     'L3_conv_dwln_g': (1.0, 0.6),
     'L3_conv_dwln_b': (0.0, 0.8),
     'L3_conv_off_b': (0.0, 0.8),
     'L3_conv_inproj_b': (0.0, 0.8),
     'L3_conv_outproj_b': (0.0, 0.1),
     'L3_conv_ln2_g': (1.0, 0.6),
     'L3_conv_ln2_b': (0.0, 2.0),
     'L3_conv_fc1_b': (0.0, 0.587),
     'L3_conv_fc2_b': (0.0, 0.267)}
    factors = {'L2_conv_qkv_w': 8.0,
     'L2_conv_rpb_table': 46.277,
     'L2_conv_proj_w': 2.855,
     'L2_conv_fc1_w': 2.99,
     'L3_conv_dw_w': 8.0,
     'L3_conv_off_w': 8.0,
     'L3_conv_mask_w': 8.0,
     'L3_conv_inproj_w': 8.0,
     'L3_conv_outproj_w': 5.373,
     'L3_conv_fc1_w': 3.022}
    for name, (base, spread) in spreads.items():
        noise = np.random.default_rng([zlib.crc32(name.encode()), seed]).standard_normal(out[name].shape)
        drawn = base * np.exp(spread * noise) if base else spread * noise
        out[name] = jnp.asarray(drawn.astype(out[name].dtype))
    for name, factor in factors.items():
        out[name] = (out[name] * factor).astype(out[name].dtype)
    return out
```

```python
from contextlib import ExitStack

import numpy as np
import concourse.bass as bass
from concourse import mybir

F32 = mybir.dt.float32
BF16 = mybir.dt.bfloat16
ALU = mybir.AluOpType
ACT = mybir.ActivationFunctionType
AX = mybir.AxisListType

B, HW, C = 32, 56, 64
T = HW * HW
ROWS = 8
CH = HW // ROWS
N = ROWS * HW
TP = 112
TILES = T // TP
TPC = N // TP
WIN = 8
NW = HW // WIN
HEADS, HD = 8, 8
G, KP = 16, 9
UNITS = G * KP
PAIRS = UNITS // 2
OBLK = UNITS * 2 // 32
FBLK = -(-UNITS // 32)
PPB = 16
WROWS = 32
LEAD = 8
CYC = 128
PASSES = 64 // WROWS
EPS = {"epsb": 1e-3, "eps2": 1e-5, "eps3": 1e-6}
PAD = HW + 2
BASE = 1
XR = 68

_COLS = [
    ("ident", 128), ("w1", 128), ("w2", 9 * 128), ("w3", 64), ("bn", 10), ("b3", 1),
    ("center", 64), ("mean", 64), ("n1w", 1), ("n1b", 1), ("n2w", 1), ("n2b", 1),
    ("wq", 128), ("wk", 128), ("wv", 128), ("bq", 1), ("bv", 64), ("dft", 64), ("idft", 64),
    ("rel", 512), ("hmask", 8), ("vmask", 128), ("floor", 1), ("zeros2", 1),
    ("proj", 64), ("projb", 1), ("fc1", 256), ("fc1b", 2), ("fc2", 128), ("fc2b", 1),
    ("l1g", 1), ("l1b", 1), ("dw", 9 * 128), ("dwb", 1), ("dwg", 1), ("dwbeta", 1),
    ("off", OBLK * 96), ("mask", UNITS), ("inw", 64), ("inb", 64), ("outw", FBLK * 64), ("outb", 1),
    ("l2g", 1), ("l2b", 1), ("f1", 256), ("f1b", 2), ("f2", 128), ("f2b", 1),
    ("epsb", 1), ("eps2", 1), ("eps3", 1), ("rowhi", 2 * CH), ("isrow", 2), ("sumy", 60), ("xneg", 1), ("yneg", CH + WROWS // 8),
]
COL = {}
_at = 0
for _name, _n in _COLS:
    COL[_name] = (_at, _n)
    _at += _n
NCOL = _at


def build(nc, x, consts, coords, selb, out):
    with ExitStack() as ctx:
        def sb(name, shape, dt=F32):
            return ctx.enter_context(nc.sbuf_tensor(name, shape, dt))

        psum = ctx.enter_context(nc.psum_tensor("psum", [128, 8, 512], F32))
        sems = {}

        def S(name):
            if name not in sems:
                sems[name] = ctx.enter_context(nc.semaphore("s_" + name))
            return sems[name]

        K = sb("consts_sb", [128, NCOL])
        SELB = sb("selb_sb", [128, 8 * 3 * 128], BF16)

        def k(name, rows=128, lo=0, n=None, row0=0):
            at, size = COL[name]
            return K[row0:row0 + rows, at + lo:at + (size if n is None else lo + n)]

        ident = k("ident")
        xN = sb("xN", [TP, TILES, C])
        shared = sb("shared", [128, T])
        xT = shared[0:C, :]
        T2 = shared[:, 0:FBLK * N].rearrange("p (f n) -> p f n", f=FBLK)
        y0T = sb("y0T", [C, T])
        y2T = y0T
        h1p = sb("h1p", [128, PAD, PAD])
        xinP = sb("xinP", [C, PAD, PAD])
        imgF = sb("imgF", [128, C, CYC])
        imgW = sb("imgW", [128, C, WROWS])
        bnp = sb("bnp", [128, 9])
        g64 = sb("g64", [C, 3 * 64 + 4])
        attnT = sb("attnT", [C, 2 * C])
        h2c = sb("h2c", [128, N])
        y1c = sb("y1c", [C, N])
        y2a = sb("y2a", [C, N])
        y2c = sb("y2c", [C, N])
        y3c = y2a
        y4c = sb("y4c", [C, N])
        xc = sb("xc", [C, N])
        sq = sb("sq", [C, N])
        rstd = sb("rstd", [C, N])
        std = sb("std", [C, N])
        xn = sb("xn", [C, N])
        ln_out = sb("ln_out", [C, N])
        dwc = y1c
        vS = sb("vS", [128, 128])
        work = sb("work", [128, 16 * N])
        area = [0]

        def take(n, rows=128):
            area[0] += n
            return work[0:rows, area[0] - n:area[0]]

        XS, xwN, qS, kS = take(N), take(N, 64), take(N), take(N)
        kexp, sS, dS, pS, pT = (take(512) for _ in range(5))
        oT = take(N, C)
        area[0] = 0
        lg, eN, mN = (take(TPC * UNITS, TP).rearrange("p (t u) -> p t u", t=TPC) for _ in range(3))
        orest = take(2 * N, 96).rearrange("p (b n) -> p b n", b=2)
        mX = take(TPC * FBLK * 128, TP).rearrange("p (t r) -> p t r", t=TPC)
        area[0] = 0
        aX, hX = (take(2 * N).rearrange("p (b n) -> p b n", b=2) for _ in range(2))
        aY, hY, prod = (take(4 * N).rearrange("p (b s n) -> p b s n", b=2, s=2) for _ in range(3))
        st = sb("st", [128, 6, 8])
        oS = sb("oS", [128, 64])
        oS2 = sb("oS2", [128, 64])
        gl = sb("gl", [128, 2, N])
        xin = sb("xin", [C, N])
        x1c = sb("x1c", [XR, N])
        ohi = sb("ohi", [96, 2, N], BF16)
        omid = sb("omid", [96, 2, N], BF16)
        O3 = sb("O3", [128, OBLK, N], BF16)
        orng = sb("orng", [32, 2 * OBLK])
        over = sb("over", [32, 2 * OBLK + 1])
        omax = sb("omax", [1, 1])
        npass = sb("npass", [1, 1], mybir.dt.int32)
        mst = sb("mst", [TP, 3, TPC * G])
        maskE = sb("maskE", [128, FBLK, N])
        ycol = sb("ycol", [128, 1])
        oN = sb("oN", [TP, TPC, C])

        def bank(b, rows=128, n=N, row0=0, at=0):
            return psum[row0:row0 + rows, b, at:at + n]

        def pair_of(b):
            return psum[:, b:b + 2, 0:N]

        def winview(ap, order):
            if order == "window":
                return ap.rearrange("p (w r c) -> p w r c", w=NW, r=ROWS)
            return ap.rearrange("p (r w c) -> p w r c", w=NW, r=ROWS)

        def bc(ap, shape):
            return ap.broadcast_to(shape)

        x_dram = x.rearrange("b (t p) c -> b p t c", p=TP)
        out_dram = out.rearrange("b (t p) c -> b p t c", p=TP)

        def pair(P):
            return [(2 * P + s) // KP for s in (0, 1)], P // 8, P // PPB

        last_pair = [min(PPB * (f + 1), PAIRS) - 1 for f in range(FBLK)]

        held = {}

        def wait_apart(eng, sem, value):
            if id(eng) not in held:
                held[id(eng)] = eng.alloc_register("awaited")
            eng.reg_add(held[id(eng)], value - 1, 1)
            eng.wait_ge(S("consts"), 32)
            eng.wait_ge(sem, held[id(eng)])

        block = ctx.enter_context(nc.Block())

        @block.sync
        def _(sp):
            sp.sem_inc(S("stored"), BASE * 16)
            sp.dma_start(K[:], consts).then_inc(S("consts"), 16)
            sp.dma_start(SELB[:], selb).then_inc(S("consts"), 16)
            with sp.Fori(0, B) as i:
                sp.wait_ge(S("gram"), BASE + i)
                sp.dma_start(xN[:], x_dram[i]).then_inc(S("xN"), 16)
                with sp.Fori(0, CH) as t:
                    c = i * CH + t
                    sp.wait_ge(S("logits"), BASE + c)
                    sp.dma_start(x1c[64:XR, :], coords[:, bass.ds(t * N, N)]).then_inc(S("coords"), 16)
                    sp.wait_ge(S("oN"), BASE + c + 1)
                    sp.dma_start(out_dram[i, :, bass.ds(t * TPC, TPC), :], oN[:]).then_inc(S("stored"), 16)
            sp.wait_ge(S("stored"), BASE * 16 + 16 * B * CH)

        @block.tensor
        def _(pe):
            pe.sem_inc(S("gram"), BASE)
            pe.sem_inc(S("logits"), BASE)
            pe.sem_inc(S("y3_ps"), BASE)
            pe.sem_inc(S("score_ps"), BASE)
            mm = nc.tensor.matmul

            def ln(name, src, c1):
                mm(bank(0, C), k("center", C), src, start=True, stop=True).then_inc(S(name + "_cen"), 1)
                wait_apart(pe, S(name + "_sq"), c1)
                mm(bank(1, C), k("mean", C), sq[:], start=True, stop=True).then_inc(S(name + "_var"), 1)

            def mlp(name, src, w1, w2, c1):
                wait_apart(pe, S(name + "_in"), c1)
                mm(bank(2), k(w1, C, 0, 128), src, start=True, stop=True)
                mm(bank(3), k(w1, C, 128, 128), src, start=True, stop=True).then_inc(S(name + "_h"), 1)
                pe.wait_ge(S(name + "_gelu"), c1)
                mm(bank(4, C), k(w2, 128, 0, 64), gl[:, 0, :], start=True, stop=False)
                mm(bank(4, C), k(w2, 128, 64, 64), gl[:, 1, :], start=False, stop=True).then_inc(S(name + "_out"), 1)

            pe.wait_ge(S("consts"), 32)
            passes = pe.alloc_register("passes_pe")
            pe.reg_mov(passes, 0)
            with pe.Fori(0, B) as i:
                pe.wait_ge(S("xN"), 16 * i + 16)
                wait_apart(pe, S("oN"), BASE + i * CH)
                for t in range(CH):
                    if t >= 2:
                        wait_apart(pe, S("xT"), i * CH + t - 1)
                    for u in range(TPC):
                        tile = t * TPC + u
                        nc.tensor.transpose(bank(1 + t % 2, C, TP, 0, TP * u), xN[:, tile, :], k("ident", TP, 0, TP)) \
                            .then_inc(S("xT_ps"), 1)
                        m = mm(bank(0, C, C), xN[:, tile, :], xN[:, tile, :], start=(tile == 0),
                               stop=(tile == TILES - 1))
                m.then_inc(S("gram"), 1)
                wait_apart(pe, S("attn"), i + 1)
                nc.tensor.transpose(bank(3, C, C), g64[:, 128:192], k("ident", C, 0, C)).then_inc(S("attnT_ps"), 1)
                wait_apart(pe, S("attnT"), i + 1)
                wait_apart(pe, S("xT"), i * CH + CH)
                with pe.Fori(0, CH) as t:
                    c = i * CH + t
                    pe.wait_ge(S("h1"), BASE + c)
                    mm(bank(0), attnT[:], xT[:, bass.ds(t * N, N)], start=True, stop=True).then_inc(S("y0_ps"), 1)
                    pe.wait_ge(S("y0"), c + 1)
                    mm(bank(1), k("w1", C), y0T[:, bass.ds(t * N, N)], start=True, stop=True).then_inc(S("h1_ps"), 1)
                wait_apart(pe, S("h1"), BASE + i * CH + CH)
                with pe.Fori(0, CH) as t:
                    c = i * CH + t
                    c1 = c + 1
                    pe.wait_ge(S("xinP"), BASE + c)
                    pe.wait_ge(S("img"), BASE + c)
                    for tap in range(9):
                        m = mm(bank(2), k("w2", 128, 128 * tap, 128),
                               h1p[:, bass.ds(t * ROWS + tap // 3, ROWS), tap % 3:tap % 3 + HW],
                               start=(tap == 0), stop=(tap == 8))
                    m.then_inc(S("h2_ps"), 1)
                    pe.wait_ge(S("h2"), c1)
                    mm(bank(3, C), k("w3"), h2c[:], start=True, stop=True).then_inc(S("y1_ps"), 1)
                    wait_apart(pe, S("y1"), c1)
                    ln("n1", y1c[:], c1)
                    wait_apart(pe, S("xs"), c1)
                    for w in range(NW):
                        m = nc.tensor.transpose(bank(2, 64, 64, 0, 64 * w), XS[0:64, 64 * w:64 * w + 64],
                                                k("ident", 64, 0, 64))
                    m.then_inc(S("xw_ps"), 1)
                    wait_apart(pe, S("xw"), c1)
                    for w in range(NW):
                        m = mm(bank(3, 64, 64, 64, 64 * w), xwN[:, 64 * w:64 * w + 64], k("dft", 64),
                               start=(w == 0), stop=(w == NW - 1), skip_group_check=True)
                    m.then_inc(S("xf_ps"), 1)
                    pe.wait_ge(S("xf"), c1)
                    mm(bank(0), k("wq"), XS, start=True, stop=True).then_inc(S("qk_ps"), 1)
                    mm(bank(1), k("wk"), XS, start=True, stop=True).then_inc(S("qk_ps"), 1)
                    pe.wait_ge(S("q"), c1)
                    for w in range(NW):
                        ws = slice(64 * w, 64 * w + 64)
                        cw = c * NW + w
                        wait_apart(pe, S("kexp"), cw + 1)
                        mm(bank(4, 64, 512), qS[0:64, ws], kexp[0:64, :], start=True, stop=True)
                        mm(bank(4, 64, 512, 64), qS[64:128, ws], kexp[64:128, :], start=True, stop=True) \
                            .then_inc(S("score_ps"), 1)
                        mm(bank(5, 64, 128), XS[:, ws], k("wv"), start=True, stop=True)
                        mm(bank(5, 64, 128, 64), XS[:, ws], k("wv"), start=True, stop=True) \
                            .then_inc(S("v_ps"), 1)
                        wait_apart(pe, S("prob"), cw + 1)
                        for hp in range(4):
                            m = nc.tensor.transpose(bank(6, 128, 128, 0, 128 * hp), pS[:, 128 * hp:128 * hp + 128], ident)
                        m.then_inc(S("probT_ps"), 1)
                        pe.wait_ge(S("probT"), cw + 1)
                        wait_apart(pe, S("v"), cw + 1)
                        for br in range(2):
                            for hp in range(4):
                                m = mm(bank(7, 64, 16, 64 * br, 16 * hp),
                                       pT[:, 128 * hp + 64 * br:128 * hp + 64 * br + 64],
                                       vS[:, 64 * br + 16 * hp:64 * br + 16 * hp + 16],
                                       start=(hp == 0), stop=(hp == 3), skip_group_check=True)
                        m.then_inc(S("o_ps"), 1)
                        pe.wait_ge(S("o"), cw + 1)
                        m = mm(bank(2, 64, 64, 0, 64 * w), oS2[:], k("idft"), start=(w == 0), stop=(w == NW - 1),
                               skip_group_check=True)
                    m.then_inc(S("oT_ps"), 1)
                    wait_apart(pe, S("oT"), c1)
                    mm(bank(3, C), k("proj", C), oT, start=True, stop=True).then_inc(S("proj_ps"), 1)
                    wait_apart(pe, S("y2a"), c1)
                    ln("n2", y2a[:], c1)
                    mlp("m2", ln_out[:], "fc1", "fc2", c1)
                    wait_apart(pe, S("y2"), c1)
                    ln("l1", y2c[:], c1)
                    wait_apart(pe, S("xin"), c1)
                    for r in range(ROWS):
                        for half in (0, 64):
                            m = mm(bank(5, HW, C, half, C * r), xin[:, HW * r:HW * r + HW], k("inw", C),
                                   start=(r == 0), stop=(r == ROWS - 1), skip_group_check=True)
                    m.then_inc(S("img_ps"), 1)
                wait_apart(pe, S("xinP"), BASE + i * CH + CH)
                with pe.Fori(0, CH) as t:
                    c = i * CH + t
                    c1 = c + 1
                    pe.wait_ge(S("oN"), BASE + c)
                    for tap in range(9):
                        m = mm(bank(2), k("dw", C, 128 * tap, 128),
                               xinP[:, bass.ds(t * ROWS + tap // 3, ROWS), tap % 3:tap % 3 + HW],
                               start=(tap == 0), stop=(tap == 8))
                    m.then_inc(S("dw_ps"), 1)
                    wait_apart(pe, S("dw"), c1)
                    ln("dl", dwc[:], c1)
                    pe.wait_ge(S("x1"), c1)
                    wait_apart(pe, S("coords"), 16 * c + 16)
                    for u in range(TPC):
                        m = mm(bank(2 + u // 2, TP, UNITS, 0, UNITS * (u % 2)), x1c[:, TP * u:TP * u + TP],
                               k("mask", XR), start=(u % 2 == 0), stop=(u % 2 == 1), skip_group_check=True)
                    m.then_inc(S("logits_ps"), 1)
                    for b in range(OBLK):
                        if b >= 2:
                            pe.wait_ge(S("orest"), c * OBLK + b - 1)
                        m = mm(bank(b % 2, 96), k("off", XR, 96 * b, 96), x1c[:], start=True, stop=True)
                        m.then_inc(S("off_ps"), 1)
                    wait_apart(pe, S("over"), c1)
                    mm(bank(7, 1, 32), over[:, 2 * OBLK:2 * OBLK + 1], k("ident", 32, 0, 32), start=True,
                       stop=True).then_inc(S("logits"), 1)
                    for f in range(FBLK):
                        pe.wait_ge(S("mX"), c1)
                        if f >= 2:
                            wait_apart(pe, S("maskE"), c * FBLK + f - 1)
                        for u in range(TPC):
                            m = nc.tensor.transpose(bank(4 + f % 2, 128, TP, 0, TP * u),
                                                    mX[:, u, 128 * f:128 * f + 128], k("ident", TP, 0, TP))
                        m.then_inc(S("mask_ps"), 1)
                    pe.wait_ge(S("osplit"), c * OBLK + OBLK)
                    pe.wait_ge(S("maskE"), c * FBLK + FBLK)
                    wait_apart(pe, S("npass"), c1)
                    todo = pe.value_load(npass[0:1, 0:1], min_val=1, max_val=PASSES)
                    with pe.Fori(0, todo) as h:
                        n = pe.snap(passes, min_val=0, max_val=PASSES * B * CH)
                        for P in range(PAIRS + 4):
                            if P < PAIRS:
                                pe.wait_ge(S("abs"), BASE + n * PAIRS + P)
                                gs, ob, f = pair(P)
                                for kind in range(3):
                                    lo = ((P % 8) * 3 + kind) * 128
                                    m = mm(bank(kind), SELB[:, lo:lo + 128], O3[:, ob, :], start=True, stop=True)
                                m.then_inc(S("spread"), 1)
                            if P >= 4:
                                R = P - 4
                                f = R // PPB
                                pe.wait_ge(S("prod"), n * PAIRS + R + 1)
                                if R % PPB == 0 and f >= 1:
                                    pe.wait_ge(S("T2"), n * FBLK + f)
                                for s in (0, 1):
                                    unit = 2 * R + s - 32 * f
                                    q, kk = unit % 4, unit // 4
                                    ks = (4 if f == FBLK - 1 else 8)
                                    m = mm(bank(7, 32, N, 32 * q), k("sumy", 128, 28 - 4 * kk, 32),
                                           prod[:, R % 2, s, :], start=(kk == 0), stop=(kk == ks - 1),
                                           tile_position=(0, 32 * q), skip_group_check=True)
                                m.then_inc(S("sumyd"), 1)
                            if 2 <= P < PAIRS + 2:
                                Q = P - 2
                                gs, ob, f = pair(Q)
                                if Q == 0:
                                    pe.wait_ge(S("imgW"), n + 1)
                                pe.wait_ge(S("hat"), n * PAIRS + Q + 1)
                                if Q >= 2:
                                    pe.wait_ge(S("prod"), n * PAIRS + Q - 1)
                                for s in (0, 1):
                                    m = mm(bank(3 + 2 * (Q % 2) + s), imgW[64 * s:64 * s + 64, 4 * gs[s]:4 * gs[s] + 4, :],
                                           hX[64 * s:64 * s + 64, Q % 2, :], start=True, stop=True)
                                m.then_inc(S("sumx"), 1)
                        pe.wait_ge(S("T2"), n * FBLK + FBLK)
                        for f in range(FBLK):
                            m = mm(bank(0, C), k("outw", 128, 64 * f, 64), T2[:, f, :], start=(f == 0),
                                   stop=(f == FBLK - 1))
                        m.then_inc(S("y3_ps"), 1)
                        pe.reg_add(passes, passes, 1)
                    wait_apart(pe, S("y3"), BASE + pe.snap(passes, min_val=1, max_val=PASSES * B * CH))
                    ln("l2", y3c[:], c1)
                    mlp("m3", ln_out[:], "f1", "f2", c1)
                    wait_apart(pe, S("y4"), c1)
                    for u in range(TPC):
                        m = nc.tensor.transpose(bank(0, TP, C, 0, C * u), y4c[:, TP * u:TP * u + TP], k("ident", C, 0, C))
                    m.then_inc(S("oN_ps"), 1)

        @block.scalar
        def _(act):
            act.sem_inc(S("abs"), BASE)
            act.sem_inc(S("h1"), BASE)
            fn = nc.scalar.activation

            def ln(name, eps, c1):
                act.wait_ge(S(name + "_cen"), c1)
                fn(xc[:], bank(0, C), ACT.Copy)
                fn(sq[:], bank(0, C), ACT.Square).then_inc(S(name + "_sq"), 1)
                act.wait_ge(S(name + "_var"), c1)
                fn(std[:], bank(1, C), ACT.Sqrt, bias=k(eps, C)).then_inc(S(name + "_sd"), 1)

            def gelu(name, b1, c1):
                act.wait_ge(S(name + "_h"), c1)
                for j in range(2):
                    m = fn(gl[:, j, :], bank(2 + j), ACT.Gelu, bias=k(b1, 128, j, 1))
                m.then_inc(S(name + "_gelu"), 1)

            act.wait_ge(S("consts"), 32)
            for j in range(2):
                fn(bnp[:, 4 + j:5 + j], k("bn", 128, 5 * j + 4, 1), ACT.Sqrt, bias=k("epsb")).then_inc(S("bnsd"), 1)
            act.wait_ge(S("bn"), 4)
            passes = act.alloc_register("passes_act")
            act.reg_mov(passes, 0)
            with act.Fori(0, B) as i:
                for t in range(CH):
                    act.wait_ge(S("xT_ps"), i * TILES + TPC * (t + 1))
                    fn(xT[:, t * N:t * N + N], bank(1 + t % 2, C), ACT.Copy).then_inc(S("xT"), 1)
                act.wait_ge(S("gmax"), i + 1)
                fn(g64[:, 0:64], bank(0, C, C), ACT.Exp, bias=g64[:, 193:194], scale=C ** -0.5,
                   accum_out=g64[:, 194:195]).then_inc(S("gexp"), 1)
                with act.Fori(0, CH) as t:
                    c = i * CH + t
                    act.wait_ge(S("y0_ps"), c + 1)
                    fn(y0T[:, bass.ds(t * N, N)], bank(0, C), ACT.Copy).then_inc(S("y0"), 1)
                    act.wait_ge(S("h1_ps"), c + 1)
                    fn(h1p[:, bass.ds(t * ROWS + 1, ROWS), 1:1 + HW], bank(1).rearrange("p (r c) -> p r c", c=HW),
                       ACT.Relu, bias=bnp[:, 1:2], scale=bnp[:, 0:1]).then_inc(S("h1"), 1)
                with act.Fori(0, CH) as t:
                    c = i * CH + t
                    c1 = c + 1
                    act.wait_ge(S("h2_ps"), c1)
                    fn(h2c[:], bank(2), ACT.Relu, bias=bnp[:, 3:4], scale=bnp[:, 2:3]).then_inc(S("h2"), 1)
                    ln("n1", "eps2", c1)
                    act.wait_ge(S("xf_ps"), c1)
                    fn(XS[64:128, :], bank(3, 64, N, 64), ACT.Copy).then_inc(S("xf"), 1)
                    act.wait_ge(S("qk_ps"), 2 * c + 2)
                    fn(kS, bank(1), ACT.Copy).then_inc(S("k"), 1)
                    for w in range(NW):
                        cw = c * NW + w
                        act.wait_ge(S("shifted"), cw + 1)
                        fn(pS, dS, ACT.Exp)
                        fn(st[:, 1, :], st[:, 0, :], ACT.Exp, scale=-1.0).then_inc(S("prob"), 1)
                        act.wait_ge(S("probT_ps"), cw + 1)
                        fn(pT, bank(6, 128, 512), ACT.Copy).then_inc(S("probT"), 1)
                    ln("n2", "eps2", c1)
                    gelu("m2", "fc1b", c1)
                    ln("l1", "eps3", c1)
                with act.Fori(0, CH) as t:
                    c = i * CH + t
                    c1 = c + 1
                    act.wait_ge(S("dw_ps"), c1)
                    fn(dwc[:], bank(2, C), ACT.Identity, bias=k("dwb", C)).then_inc(S("dw"), 1)
                    ln("dl", "eps3", c1)
                    act.wait_ge(S("dl_n"), c1)
                    fn(x1c[0:64, :], xn[:], ACT.Gelu, bias=k("dwbeta", C)).then_inc(S("x1"), 1)
                    for b in range(OBLK):
                        act.wait_ge(S("off_ps"), c * OBLK + b + 1)
                        if b >= 2:
                            act.wait_ge(S("osplit"), c * OBLK + b - 1)
                        fn(O3[0:32, b, :], bank(b % 2, 32), ACT.Copy)
                        fn(ohi[:, b % 2, :], bank(b % 2, 96), ACT.Copy).then_inc(S("ohi"), 1)
                    act.wait_ge(S("mshift"), c1)
                    fn(eN, lg, ACT.Exp).then_inc(S("mexp"), 1)
                    for f in range(FBLK):
                        act.wait_ge(S("mask_ps"), c * FBLK + f + 1)
                        fn(maskE[:, f, :], bank(4 + f % 2), ACT.Copy).then_inc(S("maskE"), 1)
                    wait_apart(act, S("npass"), c1)
                    todo = act.value_load(npass[0:1, 0:1], min_val=1, max_val=PASSES)
                    with act.Fori(0, todo) as h:
                        n = act.snap(passes, min_val=0, max_val=PASSES * B * CH)
                        act.wait_ge(S("imgW"), n + 1)
                        for P in range(PAIRS):
                            act.wait_ge(S("spread"), n * PAIRS + P + 1)
                            if P >= 2:
                                act.wait_ge(S("hat"), n * PAIRS + P - 1)
                            fn(aX[:, P % 2, :], bank(0), ACT.Abs, bias=k("xneg"))
                            fn(aY[:, P % 2], pair_of(1), ACT.Abs, bias=ycol[:]).then_inc(S("abs"), 1)
                        act.reg_add(passes, passes, 1)
                    ln("l2", "eps3", c1)
                    gelu("m3", "f1b", c1)

        @block.vector
        def _(dve):
            dve.sem_inc(S("img"), BASE)
            dve.sem_inc(S("oN"), BASE)
            dve.sem_inc(S("y3"), BASE)
            v = nc.vector

            def ln(name, gamma, c1):
                dve.wait_ge(S(name + "_sd"), c1)
                v.reciprocal(rstd[:], std[:]).then_inc(S(name + "_r"), 1)
                dve.wait_ge(S(name + "_r"), c1)
                v.scalar_tensor_tensor(xn[:], xc[:], k(gamma, C), rstd[:], ALU.mult, ALU.mult) \
                    .then_inc(S(name + "_n"), 1)

            dve.wait_ge(S("consts"), 32)
            for j in range(2):
                b_, g_, be_, m_, v_ = (k("bn", 128, 5 * j + q, 1) for q in range(5))
                dve.wait_ge(S("bnsd"), j + 1)
                v.reciprocal(bnp[:, 6 + j:7 + j], bnp[:, 4 + j:5 + j]).then_inc(S("bnt"), 1)
                v.tensor_tensor(bnp[:, 8:9], b_, m_, ALU.subtract).then_inc(S("bnt"), 1)
                dve.wait_ge(S("bnt"), 2 * j + 2)
                v.tensor_tensor(bnp[:, 2 * j:2 * j + 1], bnp[:, 6 + j:7 + j], g_, ALU.mult).then_inc(S("bn"), 1)
                dve.wait_ge(S("bn"), 2 * j + 1)
                v.scalar_tensor_tensor(bnp[:, 2 * j + 1:2 * j + 2], bnp[:, 8:9], bnp[:, 2 * j:2 * j + 1], be_,
                                       ALU.mult, ALU.add).then_inc(S("bn"), 1)
                dve.wait_ge(S("bn"), 2 * j + 2)
            v.memset(O3[96:128], 0.0).then_inc(S("cleared_rows"), 1)
            dve.wait_ge(S("cleared_rows"), 1)
            dve.wait_ge(S("cleared"), 5)
            passes = dve.alloc_register("passes_dve")
            dve.reg_mov(passes, 0)
            with dve.Fori(0, B) as i:
                dve.wait_ge(S("gram"), BASE + i + 1)
                v.tensor_reduce(g64[:, 192:193], bank(0, C, C), AX.X, ALU.max).then_inc(S("gmx"), 1)
                dve.wait_ge(S("gmx"), i + 1)
                v.tensor_scalar(g64[:, 193:194], g64[:, 192:193], -C ** -0.5, None, ALU.mult).then_inc(S("gmax"), 1)
                dve.wait_ge(S("gexp"), i + 1)
                v.reciprocal(g64[:, 195:196], g64[:, 194:195]).then_inc(S("grec"), 1)
                dve.wait_ge(S("grec"), i + 1)
                v.scalar_tensor_tensor(g64[:, 128:192], g64[:, 0:64], g64[:, 195:196], k("ident", C, 0, C),
                                       ALU.mult, ALU.add).then_inc(S("attn"), 1)
                dve.wait_ge(S("attnT_ps"), i + 1)
                v.tensor_copy(attnT[:, 0:C], bank(3, C, C)).then_inc(S("attnT"), 1)
                with dve.Fori(0, CH) as t:
                    c = i * CH + t
                    c1 = c + 1
                    dve.wait_ge(S("y1_ps"), c1)
                    v.scalar_tensor_tensor(y4c[:], bank(3, C), k("b3", C), y0T[:, bass.ds(t * N, N)], ALU.add, ALU.add) \
                        .then_inc(S("y1r"), 1)
                    dve.wait_ge(S("y1r"), c1)
                    v.tensor_scalar(y1c[:], y4c[:], 0.0, None, ALU.max).then_inc(S("y1"), 1)
                    ln("n1", "n1w", c1)
                    dve.wait_ge(S("n1_n"), c1)
                    v.tensor_scalar(winview(XS[0:64, :], "window"), winview(xn[:], "raster"), k("n1b", C), None,
                                    ALU.add).then_inc(S("xs"), 1)
                    dve.wait_ge(S("xw_ps"), c1)
                    v.tensor_copy(xwN, bank(2, 64)).then_inc(S("xw"), 1)
                    dve.wait_ge(S("qk_ps"), 2 * c + 1)
                    v.tensor_scalar(qS, bank(0), k("bq"), HD ** -0.5, ALU.add, ALU.mult).then_inc(S("q"), 1)
                    for w in range(NW):
                        cw = c * NW + w
                        dve.wait_ge(S("score_ps"), BASE + cw + 1)
                        v.tensor_tensor(sS, bank(4, 128, 512), k("rel"), ALU.add).then_inc(S("biased"), 1)
                        dve.wait_ge(S("v_ps"), cw + 1)
                        v.tensor_tensor(vS[:], bank(5, 128, 128), k("vmask"), ALU.mult).then_inc(S("v"), 1)
                        dve.wait_ge(S("biased"), cw + 1)
                        s3 = sS.rearrange("p (h m) -> p h m", h=HEADS)
                        v.tensor_reduce(st[:, 2, :], s3, AX.X, ALU.max).then_inc(S("smax"), 1)
                        dve.wait_ge(S("smax"), cw + 1)
                        v.tensor_scalar(st[:, 0, :], st[:, 2, :], k("floor"), None, ALU.max).then_inc(S("smaxf"), 1)
                        dve.wait_ge(S("smaxf"), cw + 1)
                        v.tensor_tensor(dS.rearrange("p (h m) -> p h m", h=HEADS), s3,
                                        bc(st[:, 0, :].rearrange("p (h o) -> p h o", o=1), (128, 8, 64)),
                                        ALU.subtract).then_inc(S("shifted"), 1)
                        dve.wait_ge(S("prob"), cw + 1)
                        v.tensor_reduce(st[:, 3, :], pS.rearrange("p (h m) -> p h m", h=HEADS), AX.X, ALU.add) \
                            .then_inc(S("ssum"), 1)
                        dve.wait_ge(S("ssum"), cw + 1)
                        v.scalar_tensor_tensor(st[:, 4, :], st[:, 1, :], k("zeros2"), st[:, 3, :], ALU.mult, ALU.add) \
                            .then_inc(S("ssum2"), 1)
                        dve.wait_ge(S("ssum2"), cw + 1)
                        v.reciprocal(st[:, 5, :], st[:, 4, :]).then_inc(S("srec"), 1)
                        dve.wait_ge(S("srec"), cw + 1)
                        dve.wait_ge(S("o_ps"), cw + 1)
                        v.tensor_tensor(oS[:].rearrange("p (h d) -> p h d", h=HEADS),
                                        bank(7, 128, 64).rearrange("p (h d) -> p h d", h=HEADS),
                                        bc(st[:, 5, :].rearrange("p (h o) -> p h o", o=1), (128, 8, 8)),
                                        ALU.mult).then_inc(S("on"), 1)
                        dve.wait_ge(S("on"), cw + 1)
                        v.tensor_tensor(oS2[:], oS[:], k("bv"), ALU.add).then_inc(S("o"), 1)
                    dve.wait_ge(S("oT_ps"), c1)
                    v.tensor_copy(winview(oT, "raster"), winview(bank(2, 64), "window")).then_inc(S("oT"), 1)
                    dve.wait_ge(S("proj_ps"), c1)
                    v.scalar_tensor_tensor(y2a[:], bank(3, C), k("projb", C), y1c[:], ALU.add, ALU.add) \
                        .then_inc(S("y2a"), 1)
                    ln("n2", "n2w", c1)
                    dve.wait_ge(S("n2_n"), c1)
                    v.tensor_scalar(ln_out[:], xn[:], k("n2b", C), None, ALU.add).then_inc(S("m2_in"), 1)
                    dve.wait_ge(S("m2_out"), c1)
                    v.scalar_tensor_tensor(y2c[:], bank(4, C), k("fc2b", C), y2a[:], ALU.add, ALU.add) \
                        .then_inc(S("y2"), 1)
                    ln("l1", "l1g", c1)
                    dve.wait_ge(S("l1_n"), c1)
                    v.tensor_scalar(xin[:], xn[:], k("l1b", C), None, ALU.add).then_inc(S("xin"), 1)
                    dve.wait_ge(S("img_ps"), c1)
                    inb = bc(k("inb").rearrange("p (o c) -> p o c", o=1), (128, ROWS, C))
                    src = bank(5, 128, 512).rearrange("p (r c) -> p r c", c=C)
                    for half in (0, 64):
                        for at in (LEAD, LEAD + 64):
                            dst = imgF[half:half + HW, :, bass.ds(t * ROWS + at, ROWS)].rearrange("p c r -> p r c")
                            m = v.tensor_tensor(dst, src[half:half + HW], inb[half:half + HW], ALU.add)
                    m.then_inc(S("img"), 1)
                with dve.Fori(0, CH) as t:
                    c = i * CH + t
                    c1 = c + 1
                    ln("dl", "dwg", c1)
                    dve.wait_ge(S("logits_ps"), c1)
                    for j in range(2):
                        m = v.tensor_reduce(mst[:, 0, 32 * j:32 * j + 32],
                                            bank(2 + j, TP, 2 * UNITS).rearrange("p (g q) -> p g q", q=KP),
                                            AX.X, ALU.max)
                    m.then_inc(S("mmax"), 1)
                    dve.wait_ge(S("mmax"), c1)
                    for j in range(2):
                        m = v.tensor_tensor(lg[:, 2 * j:2 * j + 2, :].rearrange("p t (g q) -> p (t g) q", q=KP),
                                            bank(2 + j, TP, 2 * UNITS).rearrange("p (g q) -> p g q", q=KP),
                                            bc(mst[:, 0, 32 * j:32 * j + 32].rearrange("p (g o) -> p g o", o=1),
                                               (TP, 32, KP)), ALU.subtract)
                    m.then_inc(S("mshift"), 1)
                    for b in range(OBLK + 1):
                        if b < OBLK:
                            dve.wait_ge(S("ohi"), c * OBLK + b + 1)
                            v.tensor_reduce(orng[:, b:b + 1], bank(b % 2, 32), AX.X, ALU.max)
                            v.tensor_reduce(orng[:, OBLK + b:OBLK + b + 1], bank(b % 2, 32), AX.X, ALU.min)
                            v.tensor_tensor(orest[:, b % 2, :], bank(b % 2, 96), ohi[:, b % 2, :], ALU.subtract) \
                                .then_inc(S("orest"), 1)
                        if b >= 1:
                            b1 = b - 1
                            dve.wait_ge(S("omid"), c * OBLK + b1 + 1)
                            v.tensor_copy(O3[32:64, b1, :], omid[32:64, b1 % 2, :])
                            v.tensor_tensor(O3[64:96, b1, :], orest[64:96, b1 % 2, :], omid[64:96, b1 % 2, :],
                                            ALU.subtract).then_inc(S("osplit"), 1)
                    dve.wait_ge(S("osplit"), c * OBLK + OBLK)
                    at = COL["rowhi"][0]
                    v.tensor_scalar(over[:, 0:OBLK], orng[:, 0:OBLK], K[0:32, bass.ds(t + at, 1)],
                                    k("isrow", 32, 0, 1), ALU.subtract, ALU.mult)
                    v.tensor_scalar(over[:, OBLK:2 * OBLK], orng[:, OBLK:2 * OBLK], K[0:32, bass.ds(t + at + CH, 1)],
                                    k("isrow", 32, 1, 1), ALU.subtract, ALU.mult).then_inc(S("over2"), 1)
                    dve.wait_ge(S("over2"), c1)
                    v.tensor_reduce(over[:, 2 * OBLK:2 * OBLK + 1], over[:, 0:2 * OBLK], AX.X, ALU.max) \
                        .then_inc(S("over"), 1)
                    dve.wait_ge(S("logits"), BASE + c1)
                    v.tensor_reduce(omax[:], bank(7, 1, 32), AX.X, ALU.max).then_inc(S("omax"), 1)
                    dve.wait_ge(S("omax"), c1)
                    v.tensor_scalar(npass[:], omax[:], 0.0, 1.0, ALU.is_gt, ALU.add).then_inc(S("npass"), 1)
                    dve.wait_ge(S("mexp"), c1)
                    e3 = eN.rearrange("p t (g q) -> p (t g) q", q=KP)
                    v.tensor_reduce(mst[:, 1, :], e3, AX.X, ALU.add).then_inc(S("msum"), 1)
                    dve.wait_ge(S("msum"), c1)
                    v.reciprocal(mst[:, 2, :], mst[:, 1, :]).then_inc(S("mrec"), 1)
                    dve.wait_ge(S("mrec"), c1)
                    v.tensor_tensor(mN.rearrange("p t (g q) -> p (t g) q", q=KP), e3,
                                    bc(mst[:, 2, :].rearrange("p (g o) -> p g o", o=1), (TP, TPC * G, KP)),
                                    ALU.mult).then_inc(S("mN"), 1)
                    dve.wait_ge(S("mN"), c1)
                    v.memset(mX[:, :, 128 * (FBLK - 1):].rearrange("p t (q r) -> p t q r", q=4)[:, :, :, 16:32], 0.0)
                    for f in range(FBLK):
                        ks = min(8, (UNITS - 32 * f) // 4)
                        for q in range(4):
                            dst = mX[:, :, 128 * f + 32 * q:128 * f + 32 * q + 4 * ks] \
                                .rearrange("p t (k c) -> p t k c", c=4)
                            src = mN[:, :, 32 * f:32 * f + 4 * ks].rearrange("p t (k c) -> p t k c", c=4)[:, :, :, q:q + 1]
                            m = v.tensor_copy(dst, bc(src, (TP, TPC, ks, 4)))
                    m.then_inc(S("mX"), 1)
                    v.tensor_scalar(y3c[:], y2T[:, bass.ds(t * N, N)], k("outb", C), None, ALU.add) \
                        .then_inc(S("y3i"), 1)
                    wait_apart(dve, S("npass"), c1)
                    todo = dve.value_load(npass[0:1, 0:1], min_val=1, max_val=PASSES)
                    with dve.Fori(0, todo) as h:
                        n = dve.snap(passes, min_val=0, max_val=PASSES * B * CH)
                        for P in range(PAIRS + 4):
                            if 2 <= P < PAIRS + 2:
                                Q = P - 2
                                dve.wait_ge(S("sumx"), n * PAIRS + Q + 1)
                                if Q >= 2:
                                    dve.wait_ge(S("sumyd"), n * PAIRS + Q - 1)
                                v.tensor_tensor(prod[:, Q % 2], pair_of(3 + 2 * (Q % 2)), hY[:, Q % 2], ALU.mult) \
                                    .then_inc(S("prod"), 1)
                            if P < PAIRS:
                                dve.wait_ge(S("abs"), BASE + n * PAIRS + P + 1)
                                if P >= 2:
                                    dve.wait_ge(S("prod"), n * PAIRS + P - 1)
                                v.tensor_scalar(hX[:, P % 2, :], aX[:, P % 2, :], 1.0, 1.0, ALU.min, ALU.subtract)
                                v.tensor_scalar(hY[:, P % 2], aY[:, P % 2], 1.0, 1.0, ALU.min, ALU.subtract) \
                                    .then_inc(S("hat"), 1)
                            if P - 4 in last_pair:
                                f = last_pair.index(P - 4)
                                dve.wait_ge(S("sumyd"), n * PAIRS + last_pair[f] + 1)
                                v.tensor_tensor(T2[:, f, :], bank(7), maskE[:, f, :], ALU.mult) \
                                    .then_inc(S("T2"), 1)
                        dve.wait_ge(S("y3_ps"), BASE + n + 1)
                        dve.wait_ge(S("y3i"), c1)
                        dve.wait_ge(S("y3"), BASE + n)
                        v.tensor_tensor(y3c[:], bank(0, C), y3c[:], ALU.add).then_inc(S("y3"), 1)
                        dve.reg_add(passes, passes, 1)
                    ln("l2", "l2g", c1)
                    dve.wait_ge(S("l2_n"), c1)
                    v.tensor_scalar(ln_out[:], xn[:], k("l2b", C), None, ALU.add).then_inc(S("m3_in"), 1)
                    dve.wait_ge(S("m3_out"), c1)
                    v.scalar_tensor_tensor(y4c[:], bank(4, C), k("f2b", C), y3c[:], ALU.add, ALU.add) \
                        .then_inc(S("y4"), 1)
                    dve.wait_ge(S("oN_ps"), c1)
                    dve.wait_ge(S("stored"), BASE * 16 + 16 * c)
                    v.tensor_copy(oN[:].rearrange("p t c -> p (t c)"), bank(0, TP, TPC * C)).then_inc(S("oN"), 1)

        @block.gpsimd
        def _(pool):
            pool.sem_inc(S("xinP"), BASE)
            g = nc.gpsimd
            g.memset(h1p[:], 0.0).then_inc(S("cleared"), 1)
            g.memset(xinP[:], 0.0).then_inc(S("cleared"), 1)
            g.memset(imgF[:], 0.0).then_inc(S("cleared"), 1)
            g.memset(attnT[:], 0.0).then_inc(S("cleared"), 1)
            g.memset(imgW[:], 0.0).then_inc(S("cleared"), 1)
            pool.wait_ge(S("cleared"), 5)
            pool.wait_ge(S("consts"), 32)
            passes = pool.alloc_register("passes_pool")
            pool.reg_mov(passes, 0)
            with pool.Fori(0, B) as i:
                with pool.Fori(0, CH) as t:
                    c = i * CH + t
                    c1 = c + 1
                    pool.wait_ge(S("k"), c1)
                    for w in range(NW):
                        cw = c * NW + w
                        pool.wait_ge(S("score_ps"), BASE + cw)
                        g.tensor_tensor(kexp.rearrange("p (h m) -> p h m", h=HEADS),
                                        bc(kS[:, 64 * w:64 * w + 64].rearrange("p (o m) -> p o m", o=1), (128, 8, 64)),
                                        bc(k("hmask").rearrange("p (h o) -> p h o", o=1), (128, 8, 64)),
                                        ALU.mult).then_inc(S("kexp"), 1)
                    wait_apart(pool, S("y2"), c1)
                    g.tensor_copy(y2T[:, bass.ds(t * N, N)], y2c[:]).then_inc(S("y2T"), 1)
                    wait_apart(pool, S("xin"), c1)
                    g.tensor_copy(xinP[:, bass.ds(t * ROWS + 1, ROWS), 1:1 + HW],
                                  xin[:].rearrange("p (r c) -> p r c", c=HW)).then_inc(S("xinP"), 1)
                with pool.Fori(0, CH) as t:
                    c = i * CH + t
                    c1 = c + 1
                    for b in range(OBLK):
                        wait_apart(pool, S("orest"), c * OBLK + b + 1)
                        if b >= 2:
                            wait_apart(pool, S("osplit"), c * OBLK + b - 1)
                        g.tensor_copy(omid[:, b % 2, :], orest[:, b % 2, :]).then_inc(S("omid"), 1)
                    wait_apart(pool, S("npass"), c1)
                    todo = pool.value_load(npass[0:1, 0:1], min_val=1, max_val=PASSES)
                    with pool.Fori(0, todo) as h:
                        n = pool.snap(passes, min_val=0, max_val=PASSES * B * CH)
                        wait_apart(pool, S("img"), BASE + i * CH + CH)
                        wait_apart(pool, S("y3_ps"), BASE + n)
                        g.tensor_copy(ycol[:], K[:, bass.ds(COL["yneg"][0] + t + h * (WROWS // 8), 1)])
                        g.tensor_copy(imgW[:], imgF[:, :, bass.ds(t * ROWS + h * WROWS, WROWS)]).then_inc(S("imgW"), 1)
                        pool.reg_add(passes, passes, 1)


def kernel(**inp):
    import numpy as np
    import ml_dtypes
    import concourse.bacc as bacc
    from concourse import mybir as mb
    from concourse.bass_utils import run_bass_kernel_spmd as run

    f = np.float32
    a = {n: np.asarray(v) for n, v in inp.items()}
    W = np.zeros((128, NCOL), f)

    def put(name, val, row0=0, lo=0):
        at, size = COL[name]
        val = val.reshape(val.shape[0], -1)
        W[row0:row0 + val.shape[0], at + lo:at + lo + val.shape[1]] = val

    col = lambda v: v.reshape(-1, 1)
    put("ident", np.eye(128, dtype=f))
    put("w1", a["L1_conv_w1"][0, 0])
    w2 = np.zeros((128, 9, 128), f)
    for g in range(32):
        w2[4 * g:4 * g + 4, :, 4 * g:4 * g + 4] = \
            a["L1_conv_w2"].reshape(9, 4, 128)[:, :, 4 * g:4 * g + 4].transpose(1, 0, 2)
    put("w2", w2)
    put("w3", a["L1_conv_w3"][0, 0])
    for j, n in enumerate(["b1", "g1", "be1", "m1", "v1", "b2", "g2", "be2", "m2", "v2"]):
        put("bn", col(a["L1_conv_" + n]), 0, j)
    put("b3", col(a["L1_conv_b3"]))
    put("center", np.eye(64, dtype=f) - f(1 / 64))
    put("mean", np.full((64, 64), 1 / 64, f))
    for n, m in [("n1w", "norm1_w"), ("n1b", "norm1_b"), ("n2w", "norm2_w"), ("n2b", "norm2_b"),
                 ("projb", "proj_b"), ("fc2b", "fc2_b")]:
        put(n, col(a["L2_conv_" + m]))
    qkv = a["L2_conv_qkv_w"]
    for br in range(2):
        for j, n in enumerate(["wq", "wk", "wv"]):
            put(n, qkv[64 * j:64 * j + 64].T, 64 * br, 64 * br)
        put("bq", col(a["L2_conv_qkv_b"][0:64]), 64 * br)
        put("bv", np.broadcast_to(a["L2_conv_qkv_b"][128:192], (64, 64)), 64 * br)
    tt = np.arange(64)[:, None]
    kr, ki = np.arange(33)[None], np.arange(1, 32)[None]
    ang = lambda kk: 2 * np.pi * ((kk * tt) % 64) / 64
    put("dft", np.concatenate([np.cos(ang(kr)), -np.sin(ang(ki))], 1).astype(f) / f(8))
    wr = np.where((kr == 0) | (kr == 32), 1.0, 2.0)
    put("idft", np.eye(64, dtype=f))
    put("idft", (np.concatenate([wr * np.cos(ang(kr)), -2 * np.sin(ang(ki))], 1) / 8).T.astype(f), 64)
    ch = np.arange(8)
    co = np.stack(np.meshgrid(ch, ch, indexing="ij")).reshape(2, -1)
    rel = (co[0][:, None] - co[0][None] + 7) * 15 + co[1][:, None] - co[1][None] + 7
    put("rel", a["L2_conv_rpb_table"][rel].transpose(0, 2, 1))
    put("hmask", np.kron(np.ones((2, 1), f), np.kron(np.eye(8, dtype=f), np.ones((8, 1), f))))
    put("vmask", np.kron(np.ones((1, 8), f), np.kron(np.eye(2, dtype=f), np.ones((64, 8), f))))
    put("floor", np.full((64, 1), -3e38, f))
    put("zeros2", np.full((64, 1), 2, f), 64)
    put("proj", a["L2_conv_proj_w"].T)
    put("fc1", a["L2_conv_fc1_w"].T)
    put("fc1b", a["L2_conv_fc1_b"].reshape(2, 128).T)
    put("fc2", a["L2_conv_fc2_w"].T.reshape(2, 128, 64).transpose(1, 0, 2))
    for n, m in [("l1g", "ln1_g"), ("l1b", "ln1_b"), ("dwb", "dw_b"), ("dwg", "dwln_g"), ("dwbeta", "dwln_b"),
                 ("outb", "outproj_b"), ("l2g", "ln2_g"), ("l2b", "ln2_b"), ("f2b", "fc2_b")]:
        put(n, col(a["L3_conv_" + m]))
    dw = np.zeros((64, 9, 128), f)
    dw[np.arange(64), :, np.arange(64)] = a["L3_conv_dw_w"].reshape(9, 64).T
    put("dw", dw)
    off = np.zeros((XR, UNITS * 2), f)
    off[0:64] = a["L3_conv_off_w"]
    off[64, 0::2] = 1
    off[65, 1::2] = 1
    off[66] = a["L3_conv_off_b"]
    pts = np.arange(UNITS) % KP
    off[67, 0::2] = pts // 3 - 1
    off[67, 1::2] = pts % 3 - 1
    put("off", np.broadcast_to(off.reshape(XR, OBLK, 1, 32), (XR, OBLK, 3, 32)))
    mk = np.zeros((XR, UNITS), f)
    mk[0:64] = a["L3_conv_mask_w"]
    mk[66] = a["L3_conv_mask_b"]
    put("mask", mk)
    put("inw", a["L3_conv_inproj_w"])
    put("inb", np.broadcast_to(a["L3_conv_inproj_b"], (128, 64)))
    ow = np.zeros((128, FBLK, 64), f)
    for u in range(UNITS):
        fb, q, kk = u // 32, u % 4, (u % 32) // 4
        ow[32 * q + 4 * kk:32 * q + 4 * kk + 4, fb] = a["L3_conv_outproj_w"][4 * (u // KP):4 * (u // KP) + 4]
    put("outw", ow)
    put("f1", a["L3_conv_fc1_w"])
    put("f1b", a["L3_conv_fc1_b"].reshape(2, 128).T)
    put("f2", a["L3_conv_fc2_w"].reshape(2, 128, 64).transpose(1, 0, 2))
    for n, e in EPS.items():
        put(n, np.full((128, 1), e, f))
    first = ROWS * np.arange(CH) - LEAD
    put("rowhi", np.broadcast_to(np.concatenate([first + WROWS - 1, first]).astype(f), (32, 2 * CH)))
    put("isrow", np.array([[j % 2, -(j % 2)] for j in range(32)], f))
    p = np.arange(128)
    sy = np.zeros((128, 60), f)
    sy[p, 28 + p // WROWS] = 1
    put("sumy", sy)
    put("xneg", -(p % 64).astype(f)[:, None])
    put("yneg", -((8 * np.arange(CH + WROWS // 8)[None] + (p % WROWS)[:, None] - LEAD) % 64).astype(f))
    coords = np.stack([np.tile(np.arange(HW), HW), np.repeat(np.arange(HW), HW), np.ones(T), np.ones(T)]).astype(f)
    sel = np.zeros((4, 32, 8, 3, 128), f)
    for j in range(8):
        sel[0:3, 4 * j, j, 0, 0:64] = 1
        sel[0:3, 4 * j + 2, j, 0, 64:128] = 1
        sel[0:3, 4 * j + 1, j, 1] = 1
        sel[0:3, 4 * j + 3, j, 2] = 1
    sel = sel.reshape(128, -1).astype(ml_dtypes.bfloat16)

    arrays = {"x_in": np.ascontiguousarray(a["x"].reshape(B, T, C)), "consts_in": W, "coords_in": coords,
              "sel_in": sel}
    nc = bacc.Bacc("TRN2", target_bir_lowering=False, num_devices=1)
    args = [nc.dram_tensor(n, v.shape, mb.dt.from_np(v.dtype), kind="ExternalInput").ap() for n, v in arrays.items()]
    o = nc.dram_tensor("out_0", (B, T, C), mb.dt.float32, kind="ExternalOutput").ap()
    build(nc, *args, o)
    r = run(nc, [arrays], core_ids=[0])
    return r.results[0]["out_0"].reshape(B, HW, HW, C)
```

```python
from contextlib import ExitStack

import numpy as np
import concourse.bass as bass
from concourse import mybir

F32 = mybir.dt.float32
BF16 = mybir.dt.bfloat16
ALU = mybir.AluOpType
ACT = mybir.ActivationFunctionType
AX = mybir.AxisListType

B, HW, C = 32, 56, 64
T = HW * HW
ROWS = 8
CH = HW // ROWS
N = ROWS * HW
TP = 112
TILES = T // TP
TPC = N // TP
WIN = 8
NW = HW // WIN
HEADS, HD = 8, 8
G, KP = 16, 9
UNITS = G * KP
PAIRS = UNITS // 2
OBLK = UNITS * 2 // 32
FBLK = -(-UNITS // 32)
PPB = 16
WROWS = 32
LEAD = 8
CYC = 128
PASSES = 64 // WROWS
EPS = {"epsb": 1e-3, "eps2": 1e-5, "eps3": 1e-6}
PAD = HW + 2
BASE = 1
XR = 68

_COLS = [
    ("ident", 128), ("w1", 128), ("w2", 9 * 128), ("w3", 64), ("bn", 10), ("b3", 1),
    ("center", 64), ("mean", 64), ("n1w", 1), ("n1b", 1), ("n2w", 1), ("n2b", 1),
    ("wq", 128), ("wk", 128), ("wv", 128), ("bq", 1), ("bv", 64), ("dft", 64), ("idft", 64),
    ("rel", 512), ("hmask", 8), ("vmask", 128), ("floor", 1), ("zeros2", 1),
    ("proj", 64), ("projb", 1), ("fc1", 256), ("fc1b", 2), ("fc2", 128), ("fc2b", 1),
    ("l1g", 1), ("l1b", 1), ("dw", 9 * 128), ("dwb", 1), ("dwg", 1), ("dwbeta", 1),
    ("off", OBLK * 96), ("mask", 2 * UNITS), ("inw", 64), ("inb", 64), ("outw", FBLK * 64), ("outb", 1),
    ("l2g", 1), ("l2b", 1), ("f1", 256), ("f1b", 2), ("f2", 128), ("f2b", 1),
    ("epsb", 1), ("eps2", 1), ("eps3", 1), ("sumy", 60), ("xneg", 1), ("yneg", CH + WROWS // 8),
]
COL = {}
_at = 0
for _name, _n in _COLS:
    COL[_name] = (_at, _n)
    _at += _n
NCOL = _at


def build(nc, x, consts, coords, selb, out):
    with ExitStack() as ctx:
        def sb(name, shape, dt=F32):
            return ctx.enter_context(nc.sbuf_tensor(name, shape, dt))

        psum = ctx.enter_context(nc.psum_tensor("psum", [128, 8, 512], F32))
        sems = {}

        def S(name):
            if name not in sems:
                sems[name] = ctx.enter_context(nc.semaphore("s_" + name))
            return sems[name]

        K = sb("consts_sb", [128, NCOL])
        SELB = sb("selb_sb", [128, 8 * 3 * 128], BF16)

        def k(name, rows=128, lo=0, n=None, row0=0):
            at, size = COL[name]
            return K[row0:row0 + rows, at + lo:at + (size if n is None else lo + n)]

        ident = k("ident")
        xN = sb("xN", [TP, TILES, C])
        shared = sb("shared", [128, T])
        xT = shared[0:C, :]
        T2 = shared[:, 0:FBLK * N].rearrange("p (f n) -> p f n", f=FBLK)
        y0T = sb("y0T", [C, T + N])
        y2T = y0T
        h1p = sb("h1p", [128, PAD + ROWS, PAD])
        xinP = sb("xinP", [C, PAD + ROWS, PAD])
        imgF = sb("imgF", [128, C, CYC])
        imgW = sb("imgW", [128, C, WROWS])
        bnp = sb("bnp", [128, 9])
        g64 = sb("g64", [C, 3 * 64 + 4])
        attnT = sb("attnT", [C, 2 * C])
        y1c = sb("y1c", [C, N])
        y2a = sb("y2a", [C, N])
        y3c = y2a
        sq = sb("sq", [C, N])
        rstd = sb("rstd", [C, N])
        std = sb("std", [C, N])
        xn = sb("xn", [C, N])
        y4c = std
        probe = sb("probe", [1, 16])
        ln_out = sb("ln_out", [C, N])
        dwc = y1c
        work = sb("work", [128, 16 * N])
        area = [0]

        def take(n, rows=128):
            area[0] += n
            return work[0:rows, area[0] - n:area[0]]

        XS, xwN, qS, kS = take(N), take(N, 64), take(N), take(N)
        sS = take(512)
        kexp, dS, pS, pT = ([take(512), take(512)] for _ in range(4))
        h2c = kexp[0][:, 0:N]
        sqN, stdN, rstdN, xnN, xin, y2c, y1t = (a[0:C, 0:N] for a in (sS, *dS, *pS, *pT))
        oT = take(N, C)
        vS = take(256).rearrange('p (b m) -> p b m', b=2)
        oS = take(64)
        area[0] = 0
        lg, eN, mN = (take(TPC * UNITS, TP).rearrange("p (t u) -> p t u", t=TPC) for _ in range(3))
        orest = take(2 * N, 96).rearrange("p (b n) -> p b n", b=2)
        mX = take(TPC * FBLK * 128, TP).rearrange("p (t r) -> p t r", t=TPC)
        sqB, stdB, rstdB, xnB = (take(N, C) for _ in range(4))
        area[0] = 0
        aX = take(2 * N).rearrange("p (b n) -> p b n", b=2)
        aY, hY = (take(4 * N).rearrange("p (b s n) -> p b s n", b=2, s=2) for _ in range(2))
        prod = take(6 * N).rearrange("p (b s n) -> p b s n", b=3, s=2)
        st = sb("st", [128, 3, 6, 8])
        oS2 = sb("oS2", [128, 2, 64])
        gl = sb("gl", [128, 2, N])
        hX = [shared[:, FBLK * N:(FBLK + 2) * N].rearrange("p (s n) -> p s n", s=2), gl]
        x1c = sb("x1c", [XR, N])
        ohi = sb("ohi", [96, 2, N], BF16)
        omid = sb("omid", [96, 2, N], BF16)
        O3 = sb("O3", [128, OBLK, N], BF16)
        orng = sb("orng", [TP, 2 * TPC])
        omax = sb("omax", [1, 1])
        npass = sb("npass", [1, 1], mybir.dt.int32)
        omost = sb("omost", [TP, 1])
        mst = sb("mst", [TP, 3, TPC * G])
        maskE = sb("maskE", [128, FBLK, N])
        ycol = sb("ycol", [128, 1])
        oN = sb("oN", [TP, TPC, C])

        def bank(b, rows=128, n=N, row0=0, at=0):
            return psum[row0:row0 + rows, b, at:at + n]

        def pair_of(b):
            return psum[:, b:b + 2, 0:N]

        def winview(ap, order):
            if order == "window":
                return ap.rearrange("p (w r c) -> p w r c", w=NW, r=ROWS)
            return ap.rearrange("p (r w c) -> p w r c", w=NW, r=ROWS)

        def bc(ap, shape):
            return ap.broadcast_to(shape)

        x_dram = x.rearrange("b (t p) c -> b p t c", p=TP)
        out_dram = out.rearrange("b (t p) c -> b p t c", p=TP)

        def pair(P):
            return [(2 * P + s) // KP for s in (0, 1)], P // 8, P // PPB

        last_pair = [min(PPB * (f + 1), PAIRS) - 1 for f in range(FBLK)]

        held = {}

        def wait_apart(eng, sem, value):
            if id(eng) not in held:
                held[id(eng)] = eng.alloc_register("awaited")
            eng.reg_add(held[id(eng)], value - 1, 1)
            eng.wait_ge(S("consts"), 32)
            eng.wait_ge(sem, held[id(eng)])

        block = ctx.enter_context(nc.Block())

        @block.sync
        def _(sp):
            sp.sem_inc(S("stored"), BASE * 16)
            sp.sem_inc(S("coords"), BASE * 16)
            sp.dma_start(K[:], consts).then_inc(S("consts"), 16)
            sp.dma_start(SELB[:], selb).then_inc(S("consts"), 16)
            with sp.Fori(0, B) as i:
                sp.wait_ge(S("gram"), BASE + i)
                sp.dma_start(xN[:], x_dram[i]).then_inc(S("xN"), 16)
                sp.wait_ge(S("coords"), BASE * 16 + 16 * (CH + 1) * i)
                sp.dma_start(x1c[64:XR, :], coords[:, 0:N]).then_inc(S("coords"), 16)
                with sp.Fori(0, CH) as t:
                    c = i * CH + t
                    sp.wait_ge(S("off_ps"), OBLK * (c + 1))
                    sp.dma_start(x1c[64:XR, :], coords[:, bass.ds((t + 1) * N, N)]).then_inc(S("coords"), 16)
                    sp.wait_ge(S("oN"), BASE + c + 1)
                    sp.dma_start(out_dram[i, :, bass.ds(t * TPC, TPC), :], oN[:]).then_inc(S("stored"), 16)
            sp.wait_ge(S("stored"), BASE * 16 + 16 * B * CH)
            sp.wait_ge(S("coords"), BASE * 16 + 16 * B * (CH + 1))

        @block.tensor
        def _(pe):
            pe.sem_inc(S("gram"), BASE)
            pe.sem_inc(S("y3_ps"), BASE)
            mm = nc.tensor.matmul

            def ln(name, src, c1):
                mm(bank(0, C), k("center", C), src, start=True, stop=True).then_inc(S(name + "_cen"), 1)
                wait_apart(pe, S(name + "_sq"), c1)
                mm(bank(1, C), k("mean", C), sq[:], start=True, stop=True).then_inc(S(name + "_var"), 1)

            def dwconv(t):
                for tap in range(9):
                    m = mm(bank(5), k("dw", C, 128 * tap, 128),
                           xinP[:, bass.ds(t * ROWS + tap // 3, ROWS), tap % 3:tap % 3 + HW],
                           start=(tap == 0), stop=(tap == 8))
                m.then_inc(S("dw_ps"), 1)

            def dwln(d1):
                wait_apart(pe, S("dw"), d1)
                mm(bank(6, C), k("center", C), dwc[:], start=True, stop=True).then_inc(S("dl_cen"), 1)
                wait_apart(pe, S("dl_sq"), d1)
                mm(bank(7, C), k("mean", C), sqB, start=True, stop=True).then_inc(S("dl_var"), 1)

            def conv(t, taps):
                for tap in taps:
                    m = mm(bank(6), k("w2", 128, 128 * tap, 128),
                           h1p[:, bass.ds(t * ROWS + tap // 3, ROWS), tap % 3:tap % 3 + HW],
                           start=(tap == 0), stop=(tap == 8))
                if 8 in taps:
                    m.then_inc(S("h2_ps"), 1)

            def conv3(d):
                pe.wait_ge(S("h2"), d)
                mm(bank(7, C), k("w3"), h2c, start=True, stop=True).then_inc(S("y1_ps"), 1)

            def n1_center(d):
                wait_apart(pe, S("y1"), d)
                mm(bank(6, C), k("center", C), y1c[:], start=True, stop=True).then_inc(S("n1_cen"), 1)

            def n1_square(d):
                wait_apart(pe, S("n1_sq"), d)
                mm(bank(7, C), k("mean", C), sqN, start=True, stop=True).then_inc(S("n1_var"), 1)

            def turn(d):
                wait_apart(pe, S("xs"), d)
                for w in range(NW):
                    m = nc.tensor.transpose(bank(6, 64, 64, 0, 64 * w), XS[0:64, 64 * w:64 * w + 64],
                                            k("ident", 64, 0, 64))
                m.then_inc(S("xw_ps"), 1)

            def fourier(d):
                wait_apart(pe, S("xw"), d)
                for w in range(NW):
                    m = mm(bank(7, 64, 64, 64, 64 * w), xwN[:, 64 * w:64 * w + 64], k("dft", 64),
                           start=(w == 0), stop=(w == NW - 1), skip_group_check=True)
                m.then_inc(S("xf_ps"), 1)

            def queries_keys(d):
                pe.wait_ge(S("xf"), d)
                mm(bank(6), k("wq"), XS, start=True, stop=True).then_inc(S("qk_ps"), 1)
                mm(bank(7), k("wk"), XS, start=True, stop=True).then_inc(S("qk_ps"), 1)

            def mlp(name, src, w1, w2, c1, between=lambda: None):
                wait_apart(pe, S(name + "_in"), c1)
                mm(bank(2), k(w1, C, 0, 128), src, start=True, stop=True)
                mm(bank(3), k(w1, C, 128, 128), src, start=True, stop=True).then_inc(S(name + "_h"), 1)
                between()
                pe.wait_ge(S(name + "_gelu"), c1)
                mm(bank(4, C), k(w2, 128, 0, 64), gl[:, 0, :], start=True, stop=False)
                mm(bank(4, C), k(w2, 128, 64, 64), gl[:, 1, :], start=False, stop=True).then_inc(S(name + "_out"), 1)

            pe.wait_ge(S("consts"), 32)
            passes = pe.alloc_register("passes_pe")
            pe.reg_mov(passes, 0)
            with pe.Fori(0, B) as i:
                pe.wait_ge(S("xN"), 16 * i + 16)
                wait_apart(pe, S("oN"), BASE + i * CH)
                for t in range(CH):
                    if t >= 2:
                        wait_apart(pe, S("xT"), i * CH + t - 1)
                    for u in range(TPC):
                        tile = t * TPC + u
                        nc.tensor.transpose(bank(1 + t % 2, C, TP, 0, TP * u), xN[:, tile, :], k("ident", TP, 0, TP)) \
                            .then_inc(S("xT_ps"), 1)
                        m = mm(bank(0, C, C), xN[:, tile, :], xN[:, tile, :], start=(tile == 0),
                               stop=(tile == TILES - 1))
                m.then_inc(S("gram"), 1)
                wait_apart(pe, S("attn"), i + 1)
                nc.tensor.transpose(bank(3, C, C), g64[:, 128:192], k("ident", C, 0, C)).then_inc(S("attnT_ps"), 1)
                wait_apart(pe, S("attnT"), i + 1)
                wait_apart(pe, S("xT"), i * CH + CH)
                for t in range(CH + 1):
                    if t < CH:
                        if t >= 2:
                            pe.wait_ge(S("y0"), i * CH + (t - 1))
                        mm(bank(t % 2), attnT[:], xT[:, t * N:t * N + N], start=True, stop=True) \
                            .then_inc(S("y0_ps"), 1)
                    if t >= 1:
                        pe.wait_ge(S("y0"), i * CH + t)
                        if t >= 3:
                            pe.wait_ge(S("h1"), i * CH + (t - 2 + BASE))
                        mm(bank(4 + (t - 1) % 2), k("w1", C), y0T[:, (t - 1) * N:t * N], start=True, stop=True) \
                            .then_inc(S("h1_ps"), 1)
                wait_apart(pe, S("h1"), BASE + i * CH + CH)
                d0 = i * (CH + 1) + 1
                conv(0, range(9))
                for step in (conv3, n1_center, n1_square, turn, fourier, queries_keys):
                    step(d0)
                with pe.Fori(0, CH) as t:
                    c = i * CH + t
                    c1 = c + 1
                    pe.wait_ge(S("xinP"), BASE + c)
                    pe.wait_ge(S("img"), BASE + c)
                    pe.wait_ge(S("q"), i * (CH + 1) + (t + 1))
                    for e in range(NW + 2):
                        if 1 <= e <= NW:
                            w = e - 1
                            wait_apart(pe, S("prob"), c * NW + (w + 1))
                            if w >= 2:
                                wait_apart(pe, S("probT"), c * NW + (w - 1))
                            for hp in range(4):
                                m = nc.tensor.transpose(bank((6, 1)[w % 2], 128, 128, 0, 128 * hp),
                                                        pS[w % 2][:, 128 * hp:128 * hp + 128], ident)
                            m.then_inc(S("probT_ps"), 1)
                        if e < NW:
                            w = e
                            ws = slice(64 * w, 64 * w + 64)
                            wait_apart(pe, S("kexp"), c * NW + (w + 1))
                            if w >= 2:
                                wait_apart(pe, S("v"), c * NW + (w - 1))
                            sc, va = ((4, 5), (0, 3))[w % 2]
                            mm(bank(sc, 64, 512), qS[0:64, ws], kexp[w % 2][0:64, :], start=True, stop=True)
                            mm(bank(sc, 64, 512, 64), qS[64:128, ws], kexp[w % 2][64:128, :], start=True, stop=True) \
                                .then_inc(S("score_ps"), 1)
                            mm(bank(va, 64, 128), XS[:, ws], k("wv"), start=True, stop=True)
                            mm(bank(va, 64, 128, 64), XS[:, ws], k("wv"), start=True, stop=True) \
                                .then_inc(S("v_ps"), 1)
                        if 1 <= e <= NW:
                            w = e - 1
                            pe.wait_ge(S("probT"), c * NW + (w + 1))
                            wait_apart(pe, S("v"), c * NW + (w + 1))
                            if w >= 1:
                                wait_apart(pe, S("on"), c * NW + w)
                            for br in range(2):
                                for hp in range(4):
                                    m = mm(bank(7, 64, 16, 64 * br, 16 * hp),
                                           pT[w % 2][:, 128 * hp + 64 * br:128 * hp + 64 * br + 64],
                                           vS[:, w % 2, 64 * br + 16 * hp:64 * br + 16 * hp + 16],
                                           start=(hp == 0), stop=(hp == 3), skip_group_check=True)
                            m.then_inc(S("o_ps"), 1)
                        if e >= 2:
                            w = e - 2
                            pe.wait_ge(S("o"), c * NW + (w + 1))
                            m = mm(bank(2, 64, 64, 0, 64 * w), oS2[:, w % 2, :], k("idft"), start=(w == 0),
                                   stop=(w == NW - 1), skip_group_check=True)
                            if w < NW - 1:
                                m.then_inc(S("idft"), 1)
                    m.then_inc(S("oT_ps"), 1)
                    d1 = pe.snap(i * (CH + 1) + (t + 2))
                    conv(t + 1, range(0, 3))
                    wait_apart(pe, S("oT"), c1)
                    mm(bank(3, C), k("proj", C), oT, start=True, stop=True).then_inc(S("proj_ps"), 1)
                    conv(t + 1, range(3, 6))
                    wait_apart(pe, S("y2a"), c1)
                    mm(bank(0, C), k("center", C), y2a[:], start=True, stop=True).then_inc(S("n2_cen"), 1)
                    conv(t + 1, range(6, 9))
                    wait_apart(pe, S("n2_sq"), c1)
                    mm(bank(1, C), k("mean", C), sq[:], start=True, stop=True).then_inc(S("n2_var"), 1)
                    conv3(d1)
                    mlp("m2", ln_out[:], "fc1", "fc2", c1, lambda: n1_center(d1))
                    n1_square(d1)
                    wait_apart(pe, S("y2"), c1)
                    ln("l1", y2c, c1)
                    turn(d1)
                    fourier(d1)
                    wait_apart(pe, S("xin"), c1)
                    for r in range(ROWS):
                        for half in (0, 64):
                            m = mm(bank(5, HW, C, half, C * r), xin[:, HW * r:HW * r + HW], k("inw", C),
                                   start=(r == 0), stop=(r == ROWS - 1), skip_group_check=True)
                    m.then_inc(S("img_ps"), 1)
                    queries_keys(d1)
                wait_apart(pe, S("xinP"), BASE + i * CH + CH)
                pe.wait_ge(S("img"), BASE + i * CH + CH)
                pe.wait_ge(S("q"), i * (CH + 1) + (CH + 1))
                dwconv(0)
                dwln(i * (CH + 1) + 1)
                with pe.Fori(0, CH) as t:
                    c = i * CH + t
                    c1 = c + 1
                    pe.wait_ge(S("oN"), BASE + c)
                    pe.wait_ge(S("x1"), i * (CH + 1) + (t + 1))
                    wait_apart(pe, S("coords"), (i * (CH + 1) + t) * 16 + (16 + BASE * 16))
                    for u in range(TPC):
                        m = mm(bank(4 + u, TP, 2 * UNITS), x1c[:, TP * u:TP * u + TP], k("mask", XR),
                               start=True, stop=True)
                    m.then_inc(S("logits_ps"), 1)
                    for b in range(OBLK):
                        if b >= 4:
                            pe.wait_ge(S("orest"), c * OBLK + b - 3)
                        m = mm(bank(b % 4, 96), k("off", XR, 96 * b, 96), x1c[:], start=True, stop=True)
                        m.then_inc(S("off_ps"), 1)
                        if b == 3:
                            wait_apart(pe, S("omost"), c1)
                            mm(bank(7, 1, TP), omost[:], k("ident", TP, 0, TP), start=True, stop=True) \
                                .then_inc(S("omost_ps"), 1)
                    for f in range(FBLK):
                        pe.wait_ge(S("mX"), c1)
                        if f >= 2:
                            wait_apart(pe, S("maskE"), c * FBLK + f - 1)
                        for u in range(TPC):
                            m = nc.tensor.transpose(bank(4 + f % 2, 128, TP, 0, TP * u),
                                                    mX[:, u, 128 * f:128 * f + 128], k("ident", TP, 0, TP))
                        m.then_inc(S("mask_ps"), 1)
                    pe.wait_ge(S("osplit"), c * OBLK + OBLK)
                    pe.wait_ge(S("maskE"), c * FBLK + FBLK)
                    wait_apart(pe, S("npass"), c1)
                    todo = pe.value_load(npass[0:1, 0:1], min_val=1, max_val=PASSES)
                    with pe.Fori(0, todo) as h:
                        n = pe.snap(passes, min_val=0, max_val=PASSES * B * CH)
                        pe.wait_ge(S("y3"), n + BASE)
                        for P in range(PAIRS + 4):
                            if P < PAIRS:
                                pe.wait_ge(S("absx"), n * PAIRS + (P + BASE))
                                gs, ob, f = pair(P)
                                for kind in range(3):
                                    if kind == 1:
                                        pe.wait_ge(S("abs"), n * PAIRS + (P + BASE))
                                    lo = ((P % 8) * 3 + kind) * 128
                                    m = mm(bank(kind), SELB[:, lo:lo + 128], O3[:, ob, :], start=True, stop=True)
                                    if kind == 0:
                                        m.then_inc(S("spreadx"), 1)
                                m.then_inc(S("spread"), 1)
                            if 2 <= P < PAIRS + 2:
                                Q = P - 2
                                gs, ob, f = pair(Q)
                                if Q == 0:
                                    pe.wait_ge(S("imgW"), n + 1)
                                pe.wait_ge(S("hat"), n * PAIRS + Q + 1)
                                if Q >= 2:
                                    pe.wait_ge(S("prod"), n * PAIRS + Q - 1)
                                for s in (0, 1):
                                    m = mm(bank(3 + 2 * (Q % 2) + s), imgW[:, 4 * gs[s]:4 * gs[s] + 4, :],
                                           hX[Q % 2][:, s, :], start=True, stop=True)
                                m.then_inc(S("sumx"), 1)
                            if P >= 4 and P % 2 == 0:
                                for R in (P - 4, P - 3):
                                    f = R // PPB
                                    pe.wait_ge(S("prod"), n * PAIRS + R + 1)
                                    if R % PPB == 0 and f >= 1:
                                        pe.wait_ge(S("T2"), n * FBLK + f)
                                    for s in (0, 1):
                                        unit = 2 * R + s - 32 * f
                                        q, kk = unit % 4, unit // 4
                                        ks = (4 if f == FBLK - 1 else 8)
                                        m = mm(bank(7, 32, N, 32 * q), k("sumy", 128, 28 - 4 * kk, 32),
                                               prod[:, R % 3, s, :], start=(kk == 0), stop=(kk == ks - 1),
                                               tile_position=(0, 32 * q), skip_group_check=True)
                                    m.then_inc(S("sumyd"), 1)
                        pe.wait_ge(S("T2"), n * FBLK + FBLK)
                        for f in range(FBLK):
                            m = mm(bank(0, C), k("outw", 128, 64 * f, 64), T2[:, f, :], start=(f == 0),
                                   stop=(f == FBLK - 1))
                        m.then_inc(S("y3_ps"), 1)
                        pe.reg_add(passes, passes, 1)
                    wait_apart(pe, S("y3"), BASE + pe.snap(passes, min_val=1, max_val=PASSES * B * CH))
                    mm(bank(0, C), k("center", C), y3c[:], start=True, stop=True).then_inc(S("l2_cen"), 1)
                    d1 = pe.snap(i * (CH + 1) + (t + 2))
                    dwconv(t + 1)
                    wait_apart(pe, S("l2_sq"), c1)
                    mm(bank(1, C), k("mean", C), sq[:], start=True, stop=True).then_inc(S("l2_var"), 1)
                    dwln(d1)
                    mlp("m3", ln_out[:], "f1", "f2", c1)
                    wait_apart(pe, S("y4"), c1)
                    for u in range(TPC):
                        m = nc.tensor.transpose(bank(0, TP, C, 0, C * u), y4c[:, TP * u:TP * u + TP], k("ident", C, 0, C))
                    m.then_inc(S("oN_ps"), 1)

        @block.scalar
        def _(act):
            act.sem_inc(S("abs"), BASE)
            act.sem_inc(S("absx"), BASE)
            act.sem_inc(S("h1"), BASE)
            fn = nc.scalar.activation

            cells = iter(range(16))

            def set_for(func):
                cell = next(cells)
                fn(probe[:, cell:cell + 1], k("eps2", 1), func)

            def ln(name, eps, c1):
                act.wait_ge(S(name + "_cen"), c1)
                fn(sq[:], bank(0, C), ACT.Square).then_inc(S(name + "_sq"), 1)
                set_for(ACT.Ln)
                act.wait_ge(S(name + "_var"), c1)
                fn(std[:], bank(1, C), ACT.Ln, bias=k(eps, C)).then_inc(S(name + "_ln"), 1)
                act.wait_ge(S(name + "_ln"), c1)
                fn(rstd[:], std[:], ACT.Exp, scale=-0.5).then_inc(S(name + "_r"), 1)

            def gelu(name, b1, c1):
                set_for(ACT.Gelu)
                act.wait_ge(S(name + "_h"), c1)
                for j in range(2):
                    m = fn(gl[:, j, :], bank(2 + j), ACT.Gelu, bias=k(b1, 128, j, 1))
                m.then_inc(S(name + "_gelu"), 1)

            def h2(d):
                act.wait_ge(S("h2_ps"), d)
                fn(h2c, bank(6), ACT.Relu, bias=bnp[:, 3:4], scale=bnp[:, 2:3]).then_inc(S("h2"), 1)

            def n1(d):
                act.wait_ge(S("n1_cen"), d)
                fn(sqN, bank(6, C), ACT.Square).then_inc(S("n1_sq"), 1)
                act.wait_ge(S("n1_var"), d)
                fn(stdN, bank(7, C), ACT.Ln, bias=k("eps2", C)).then_inc(S("n1_ln"), 1)
                act.wait_ge(S("n1_ln"), d)
                fn(rstdN, stdN, ACT.Exp, scale=-0.5).then_inc(S("n1_r"), 1)

            def keys(d):
                act.wait_ge(S("xf_ps"), d)
                fn(XS[64:128, :], bank(7, 64, N, 64), ACT.Copy).then_inc(S("xf"), 1)
                act.wait_ge(S("qk_ps"), 2 * d)
                fn(kS, bank(7), ACT.Copy).then_inc(S("k"), 1)

            def dwsq(d1):
                act.wait_ge(S("dl_cen"), d1)
                fn(sqB, bank(6, C), ACT.Square).then_inc(S("dl_sq"), 1)
                act.wait_ge(S("dl_var"), d1)
                fn(stdB, bank(7, C), ACT.Ln, bias=k("eps3", C)).then_inc(S("dl_ln"), 1)
                act.wait_ge(S("dl_ln"), d1)
                fn(rstdB, stdB, ACT.Exp, scale=-0.5).then_inc(S("dl_r"), 1)

            def dwbias(d1):
                act.wait_ge(S("dw_ps"), d1)
                fn(dwc[:], bank(5, C), ACT.Identity, bias=k("dwb", C)).then_inc(S("dw"), 1)

            def x1(d1):
                act.wait_ge(S("dl_n"), d1)
                fn(x1c[0:64, :], xnB, ACT.Gelu, bias=k("dwbeta", C)).then_inc(S("x1"), 1)

            act.wait_ge(S("consts"), 32)
            for j in range(2):
                fn(bnp[:, 4 + j:5 + j], k("bn", 128, 5 * j + 4, 1), ACT.Sqrt, bias=k("epsb")).then_inc(S("bnsd"), 1)
            act.wait_ge(S("bn"), 4)
            passes = act.alloc_register("passes_act")
            act.reg_mov(passes, 0)
            with act.Fori(0, B) as i:
                for t in range(CH):
                    act.wait_ge(S("xT_ps"), i * TILES + TPC * (t + 1))
                    fn(xT[:, t * N:t * N + N], bank(1 + t % 2, C), ACT.Copy).then_inc(S("xT"), 1)
                act.wait_ge(S("gmax"), i + 1)
                fn(g64[:, 0:64], bank(0, C, C), ACT.Exp, bias=g64[:, 193:194], scale=C ** -0.5,
                   accum_out=g64[:, 194:195]).then_inc(S("gexp"), 1)
                for t in range(CH + 1):
                    if t < CH:
                        act.wait_ge(S("y0_ps"), i * CH + (t + 1))
                        fn(y0T[:, t * N:t * N + N], bank(t % 2, C), ACT.Copy).then_inc(S("y0"), 1)
                    if t >= 1:
                        act.wait_ge(S("h1_ps"), i * CH + t)
                        fn(h1p[:, (t - 1) * ROWS + 1:t * ROWS + 1, 1:1 + HW],
                           bank(4 + (t - 1) % 2).rearrange("p (r c) -> p r c", c=HW),
                           ACT.Relu, bias=bnp[:, 1:2], scale=bnp[:, 0:1]).then_inc(S("h1"), 1)
                d0 = i * (CH + 1) + 1
                for step in (h2, n1, keys):
                    step(d0)
                with act.Fori(0, CH) as t:
                    c = i * CH + t
                    c1 = c + 1
                    act.wait_ge(S("xinP"), BASE + c)
                    for e in range(NW + 1):
                        if e >= 1:
                            w = e - 1
                            act.wait_ge(S("probT_ps"), c * NW + (w + 1))
                            if w >= 2:
                                act.wait_ge(S("o_ps"), c * NW + (w - 1))
                            fn(pT[w % 2], bank((6, 1)[w % 2], 128, 512), ACT.Copy).then_inc(S("probT"), 1)
                        if e < NW:
                            w = e
                            act.wait_ge(S("shifted"), c * NW + (w + 1))
                            if w >= 2:
                                act.wait_ge(S("ssum"), c * NW + (w - 1))
                            fn(pS[w % 2], dS[w % 2], ACT.Exp)
                            fn(st[:, w % 3, 1, :], st[:, w % 3, 0, :], ACT.Exp, scale=-1.0).then_inc(S("prob"), 1)
                    d1 = act.snap(i * (CH + 1) + (t + 2))
                    act.wait_ge(S("n2_cen"), c1)
                    fn(sq[:], bank(0, C), ACT.Square).then_inc(S("n2_sq"), 1)
                    h2(d1)
                    act.wait_ge(S("n2_var"), c1)
                    fn(std[:], bank(1, C), ACT.Ln, bias=k("eps2", C)).then_inc(S("n2_ln"), 1)
                    act.wait_ge(S("n2_ln"), c1)
                    fn(rstd[:], std[:], ACT.Exp, scale=-0.5).then_inc(S("n2_r"), 1)
                    gelu("m2", "fc1b", c1)
                    n1(d1)
                    ln("l1", "eps3", c1)
                    keys(d1)
                dwbias(i * (CH + 1) + 1)
                dwsq(i * (CH + 1) + 1)
                x1(i * (CH + 1) + 1)
                with act.Fori(0, CH) as t:
                    c = i * CH + t
                    c1 = c + 1
                    set_for(ACT.Exp)
                    for b in range(OBLK + 1):
                        if b < OBLK:
                            act.wait_ge(S("off_ps"), c * OBLK + b + 1)
                            if b >= 2:
                                act.wait_ge(S("orest"), c * OBLK + b - 1)
                            fn(O3[0:32, b, :], bank(b % 4, 32), ACT.Copy)
                            fn(ohi[:, b % 2, :], bank(b % 4, 96), ACT.Copy).then_inc(S("ohi"), 1)
                        if b == 1:
                            act.wait_ge(S("mshift"), c1)
                            fn(eN, lg, ACT.Exp).then_inc(S("mexp"), 1)
                        if b >= 1:
                            act.wait_ge(S("orest"), c * OBLK + b)
                            if b >= 3:
                                act.wait_ge(S("osplit"), c * OBLK + b - 2)
                            fn(omid[:, (b - 1) % 2, :], orest[:, (b - 1) % 2, :], ACT.Copy).then_inc(S("omid"), 1)
                    for f in range(FBLK):
                        act.wait_ge(S("mask_ps"), c * FBLK + f + 1)
                        fn(maskE[:, f, :], bank(4 + f % 2), ACT.Copy).then_inc(S("maskE"), 1)
                    wait_apart(act, S("npass"), c1)
                    todo = act.value_load(npass[0:1, 0:1], min_val=1, max_val=PASSES)
                    with act.Fori(0, todo) as h:
                        n = act.snap(passes, min_val=0, max_val=PASSES * B * CH)
                        act.wait_ge(S("imgW"), n + 1)
                        for P in range(PAIRS):
                            act.wait_ge(S("spreadx"), n * PAIRS + P + 1)
                            if P >= 2:
                                act.wait_ge(S("hat"), n * PAIRS + P - 1)
                            fn(aX[:, P % 2, :], bank(0), ACT.Abs, bias=k("xneg")).then_inc(S("absx"), 1)
                            act.wait_ge(S("spread"), n * PAIRS + P + 1)
                            fn(aY[:, P % 2], pair_of(1), ACT.Abs, bias=ycol[:]).then_inc(S("abs"), 1)
                        act.reg_add(passes, passes, 1)
                    d1 = act.snap(i * (CH + 1) + (t + 2))
                    act.wait_ge(S("l2_cen"), c1)
                    fn(sq[:], bank(0, C), ACT.Square).then_inc(S("l2_sq"), 1)
                    set_for(ACT.Ln)
                    dwbias(d1)
                    act.wait_ge(S("l2_var"), c1)
                    fn(std[:], bank(1, C), ACT.Ln, bias=k("eps3", C)).then_inc(S("l2_ln"), 1)
                    act.wait_ge(S("l2_ln"), c1)
                    fn(rstd[:], std[:], ACT.Exp, scale=-0.5).then_inc(S("l2_r"), 1)
                    dwsq(d1)
                    gelu("m3", "f1b", c1)
                    x1(d1)

        @block.vector
        def _(dve):
            dve.sem_inc(S("img"), BASE)
            dve.sem_inc(S("oN"), BASE)
            dve.sem_inc(S("y3"), BASE)
            v = nc.vector

            def ln(name, gamma, c1):
                dve.wait_ge(S(name + "_r"), c1)
                v.scalar_tensor_tensor(xn[:], bank(0, C), k(gamma, C), rstd[:], ALU.mult, ALU.mult) \
                    .then_inc(S(name + "_n"), 1)

            def dwnorm(d1):
                dve.wait_ge(S("dl_r"), d1)
                v.scalar_tensor_tensor(xnB, bank(6, C), k("dwg", C), rstdB, ALU.mult, ALU.mult) \
                    .then_inc(S("dl_n"), 1)

            def residual(t, d):
                dve.wait_ge(S("y1_ps"), d)
                v.scalar_tensor_tensor(y1t, bank(7, C), k("b3", C), y0T[:, bass.ds(t * N, N)], ALU.add, ALU.add) \
                    .then_inc(S("y1r"), 1)
                dve.wait_ge(S("y1r"), d)
                v.tensor_scalar(y1c[:], y1t, 0.0, None, ALU.max).then_inc(S("y1"), 1)

            def windows_in(d):
                dve.wait_ge(S("n1_r"), d)
                v.scalar_tensor_tensor(xnN, bank(6, C), k("n1w", C), rstdN, ALU.mult, ALU.mult).then_inc(S("n1_n"), 1)
                dve.wait_ge(S("n1_n"), d)
                v.tensor_scalar(winview(XS[0:64, :], "window"), winview(xnN, "raster"), k("n1b", C), None,
                                ALU.add).then_inc(S("xs"), 1)

            def turned(d):
                dve.wait_ge(S("xw_ps"), d)
                v.tensor_copy(xwN, bank(6, 64)).then_inc(S("xw"), 1)

            def queries(d):
                dve.wait_ge(S("qk_ps"), 2 * d - 1)
                v.tensor_scalar(qS, bank(6), k("bq"), HD ** -0.5, ALU.add, ALU.mult).then_inc(S("q"), 1)

            dve.wait_ge(S("consts"), 32)
            for j in range(2):
                b_, g_, be_, m_, v_ = (k("bn", 128, 5 * j + q, 1) for q in range(5))
                dve.wait_ge(S("bnsd"), j + 1)
                v.reciprocal(bnp[:, 6 + j:7 + j], bnp[:, 4 + j:5 + j]).then_inc(S("bnt"), 1)
                v.tensor_tensor(bnp[:, 8:9], b_, m_, ALU.subtract).then_inc(S("bnt"), 1)
                dve.wait_ge(S("bnt"), 2 * j + 2)
                v.tensor_tensor(bnp[:, 2 * j:2 * j + 1], bnp[:, 6 + j:7 + j], g_, ALU.mult).then_inc(S("bn"), 1)
                dve.wait_ge(S("bn"), 2 * j + 1)
                v.scalar_tensor_tensor(bnp[:, 2 * j + 1:2 * j + 2], bnp[:, 8:9], bnp[:, 2 * j:2 * j + 1], be_,
                                       ALU.mult, ALU.add).then_inc(S("bn"), 1)
                dve.wait_ge(S("bn"), 2 * j + 2)
            v.memset(O3[96:128], 0.0).then_inc(S("cleared_rows"), 1)
            dve.wait_ge(S("cleared_rows"), 1)
            dve.wait_ge(S("cleared"), 6)
            passes = dve.alloc_register("passes_dve")
            dve.reg_mov(passes, 0)
            with dve.Fori(0, B) as i:
                dve.wait_ge(S("gram"), BASE + i + 1)
                v.tensor_reduce(g64[:, 192:193], bank(0, C, C), AX.X, ALU.max).then_inc(S("gmx"), 1)
                dve.wait_ge(S("gmx"), i + 1)
                v.tensor_scalar(g64[:, 193:194], g64[:, 192:193], -C ** -0.5, None, ALU.mult).then_inc(S("gmax"), 1)
                dve.wait_ge(S("gexp"), i + 1)
                v.reciprocal(g64[:, 195:196], g64[:, 194:195]).then_inc(S("grec"), 1)
                dve.wait_ge(S("grec"), i + 1)
                v.scalar_tensor_tensor(g64[:, 128:192], g64[:, 0:64], g64[:, 195:196], k("ident", C, 0, C),
                                       ALU.mult, ALU.add).then_inc(S("attn"), 1)
                dve.wait_ge(S("attnT_ps"), i + 1)
                v.tensor_copy(attnT[:, 0:C], bank(3, C, C)).then_inc(S("attnT"), 1)
                d0 = i * (CH + 1) + 1
                residual(0, d0)
                for step in (windows_in, turned, queries):
                    step(d0)
                with dve.Fori(0, CH) as t:
                    c = i * CH + t
                    c1 = c + 1
                    by_head = lambda ap: ap.rearrange("p (h m) -> p h m", h=HEADS)
                    for e in range(NW + 2):
                        if e >= 2:
                            w = e - 2
                            dve.wait_ge(S("o_ps"), c * NW + (w + 1))
                            dve.wait_ge(S("srec"), c * NW + (w + 1))
                            if w >= 1:
                                dve.wait_ge(S("o"), c * NW + w)
                            v.tensor_tensor(by_head(oS), by_head(bank(7, 128, 64)),
                                            bc(st[:, w % 3, 5, :].rearrange("p (h o) -> p h o", o=1), (128, 8, 8)),
                                            ALU.mult).then_inc(S("on"), 1)
                            dve.wait_ge(S("on"), c * NW + (w + 1))
                            if w >= 2:
                                dve.wait_ge(S("idft"), c * (NW - 1) + (w - 1))
                            v.tensor_tensor(oS2[:, w % 2, :], oS, k("bv"), ALU.add).then_inc(S("o"), 1)
                        if e < NW:
                            w = e
                            dve.wait_ge(S("score_ps"), c * NW + (w + 1))
                            if w >= 1:
                                dve.wait_ge(S("shifted"), c * NW + w)
                            v.tensor_tensor(sS, bank((4, 0)[w % 2], 128, 512), k("rel"), ALU.add).then_inc(S("biased"), 1)
                            dve.wait_ge(S("v_ps"), c * NW + (w + 1))
                            if w >= 2:
                                dve.wait_ge(S("o_ps"), c * NW + (w - 1))
                            v.tensor_tensor(vS[:, w % 2, :], bank((5, 3)[w % 2], 128, 128), k("vmask"), ALU.mult) \
                                .then_inc(S("v"), 1)
                            dve.wait_ge(S("biased"), c * NW + (w + 1))
                            if w >= 3:
                                dve.wait_ge(S("on"), c * NW + (w - 2))
                            v.tensor_reduce(st[:, w % 3, 2, :], by_head(sS), AX.X, ALU.max).then_inc(S("smax"), 1)
                            dve.wait_ge(S("smax"), c * NW + (w + 1))
                            v.tensor_scalar(st[:, w % 3, 0, :], st[:, w % 3, 2, :], k("floor"), None, ALU.max) \
                                .then_inc(S("smaxf"), 1)
                            dve.wait_ge(S("smaxf"), c * NW + (w + 1))
                            if w >= 2:
                                dve.wait_ge(S("prob"), c * NW + (w - 1))
                            v.tensor_tensor(by_head(dS[w % 2]), by_head(sS),
                                            bc(st[:, w % 3, 0, :].rearrange("p (h o) -> p h o", o=1), (128, 8, 64)),
                                            ALU.subtract).then_inc(S("shifted"), 1)
                        if 1 <= e <= NW:
                            w = e - 1
                            dve.wait_ge(S("prob"), c * NW + (w + 1))
                            v.tensor_reduce(st[:, w % 3, 3, :], by_head(pS[w % 2]), AX.X, ALU.add).then_inc(S("ssum"), 1)
                            dve.wait_ge(S("ssum"), c * NW + (w + 1))
                            v.scalar_tensor_tensor(st[:, w % 3, 4, :], st[:, w % 3, 1, :], k("zeros2"),
                                                   st[:, w % 3, 3, :], ALU.mult, ALU.add).then_inc(S("ssum2"), 1)
                            dve.wait_ge(S("ssum2"), c * NW + (w + 1))
                            v.reciprocal(st[:, w % 3, 5, :], st[:, w % 3, 4, :]).then_inc(S("srec"), 1)
                    dve.wait_ge(S("oT_ps"), c1)
                    v.tensor_copy(winview(oT, "raster"), winview(bank(2, 64), "window")).then_inc(S("oT"), 1)
                    dve.wait_ge(S("proj_ps"), c1)
                    v.scalar_tensor_tensor(y2a[:], bank(3, C), k("projb", C), y1c[:], ALU.add, ALU.add) \
                        .then_inc(S("y2a"), 1)
                    d1 = dve.snap(i * (CH + 1) + (t + 2))
                    ln("n2", "n2w", c1)
                    dve.wait_ge(S("n2_n"), c1)
                    v.tensor_scalar(ln_out[:], xn[:], k("n2b", C), None, ALU.add).then_inc(S("m2_in"), 1)
                    dve.wait_ge(S("y2a"), c1)
                    residual(t + 1, d1)
                    dve.wait_ge(S("m2_out"), c1)
                    v.scalar_tensor_tensor(y2c, bank(4, C), k("fc2b", C), y2a[:], ALU.add, ALU.add) \
                        .then_inc(S("y2"), 1)
                    windows_in(d1)
                    ln("l1", "l1g", c1)
                    dve.wait_ge(S("l1_n"), c1)
                    v.tensor_scalar(xin, xn[:], k("l1b", C), None, ALU.add).then_inc(S("xin"), 1)
                    turned(d1)
                    dve.wait_ge(S("img_ps"), c1)
                    inb = bc(k("inb").rearrange("p (o c) -> p o c", o=1), (128, ROWS, C))
                    src = bank(5, 128, 512).rearrange("p (r c) -> p r c", c=C)
                    for half in (0, 64):
                        for at in (LEAD, LEAD + 64):
                            dst = imgF[half:half + HW, :, bass.ds(t * ROWS + at, ROWS)].rearrange("p c r -> p r c")
                            m = v.tensor_tensor(dst, src[half:half + HW], inb[half:half + HW], ALU.add)
                    m.then_inc(S("img"), 1)
                    queries(d1)
                dwnorm(i * (CH + 1) + 1)
                with dve.Fori(0, CH) as t:
                    c = i * CH + t
                    c1 = c + 1
                    dve.wait_ge(S("logits_ps"), c1)
                    by_group = lambda ap: ap.rearrange("p t (g q) -> p t g q", q=KP)
                    logits = by_group(psum[0:TP, 4:4 + TPC, 0:UNITS])
                    spread9 = lambda a: bc(mst[:, a, :].rearrange("p (t g o) -> p t g o", t=TPC, o=1), (TP, TPC, G, KP))
                    v.tensor_reduce(mst[:, 0, :].rearrange("p (t g) -> p t g", t=TPC), logits, AX.X, ALU.max) \
                        .then_inc(S("mmax"), 1)
                    dve.wait_ge(S("mmax"), c1)
                    v.tensor_tensor(by_group(lg), logits, spread9(0), ALU.subtract).then_inc(S("mshift"), 1)
                    rows = psum[0:TP, 4:4 + TPC, UNITS:2 * UNITS]
                    v.tensor_reduce(orng[:, 0:TPC], rows, AX.X, ALU.max)
                    v.tensor_reduce(orng[:, TPC:], rows, AX.X, ALU.min).then_inc(S("orng"), 1)
                    dve.wait_ge(S("orng"), c1)
                    v.tensor_scalar(orng[:, TPC:], orng[:, TPC:], -1.0, None, ALU.mult).then_inc(S("orneg"), 1)
                    dve.wait_ge(S("orneg"), c1)
                    v.tensor_reduce(omost[:], orng[:], AX.X, ALU.max).then_inc(S("omost"), 1)
                    for b in range(OBLK + 1):
                        if b < OBLK:
                            dve.wait_ge(S("ohi"), c * OBLK + b + 1)
                            if b >= 2:
                                dve.wait_ge(S("osplit"), c * OBLK + b - 1)
                            v.tensor_tensor(orest[:, b % 2, :], bank(b % 4, 96), ohi[:, b % 2, :], ALU.subtract) \
                                .then_inc(S("orest"), 1)
                        if b >= 1:
                            b1 = b - 1
                            dve.wait_ge(S("omid"), c * OBLK + b1 + 1)
                            v.tensor_copy(O3[32:64, b1, :], omid[32:64, b1 % 2, :])
                            v.tensor_tensor(O3[64:96, b1, :], orest[64:96, b1 % 2, :], omid[64:96, b1 % 2, :],
                                            ALU.subtract).then_inc(S("osplit"), 1)
                        if b == 3:
                            dve.wait_ge(S("omost_ps"), c1)
                            v.tensor_reduce(omax[:], bank(7, 1, TP), AX.X, ALU.max).then_inc(S("omax"), 1)
                            dve.wait_ge(S("omax"), c1)
                            v.tensor_scalar(npass[:], omax[:], float(LEAD - 1), 1.0, ALU.is_gt, ALU.add) \
                                .then_inc(S("npass"), 1)
                        if b == 2:
                            dve.wait_ge(S("mexp"), c1)
                            v.tensor_reduce(mst[:, 1, :].rearrange("p (t g) -> p t g", t=TPC), by_group(eN), AX.X,
                                            ALU.add).then_inc(S("msum"), 1)
                            dve.wait_ge(S("msum"), c1)
                            v.reciprocal(mst[:, 2, :], mst[:, 1, :]).then_inc(S("mrec"), 1)
                            dve.wait_ge(S("mrec"), c1)
                            v.tensor_tensor(by_group(mN), by_group(eN), spread9(2), ALU.mult).then_inc(S("mN"), 1)
                            dve.wait_ge(S("mN"), c1)
                            v.memset(mX[:, :, 128 * (FBLK - 1):].rearrange("p t (q r) -> p t q r", q=4)[:, :, :, 16:32],
                                     0.0)
                            for f in range(FBLK):
                                ks = min(8, (UNITS - 32 * f) // 4)
                                for q in range(4):
                                    dst = mX[:, :, 128 * f + 32 * q:128 * f + 32 * q + 4 * ks] \
                                        .rearrange("p t (k c) -> p t k c", c=4)
                                    src = mN[:, :, 32 * f:32 * f + 4 * ks] \
                                        .rearrange("p t (k c) -> p t k c", c=4)[:, :, :, q:q + 1]
                                    m = v.tensor_copy(dst, bc(src, (TP, TPC, ks, 4)))
                            m.then_inc(S("mX"), 1)
                    for b in range(2):
                        v.memset(hX[b][64:128, 0, :], 0.0)
                        v.memset(hX[b][0:64, 1, :], 0.0)
                    v.tensor_scalar(y3c[:], y2T[:, bass.ds(t * N, N)], k("outb", C), None, ALU.add) \
                        .then_inc(S("y3i"), 1)
                    wait_apart(dve, S("npass"), c1)
                    todo = dve.value_load(npass[0:1, 0:1], min_val=1, max_val=PASSES)
                    with dve.Fori(0, todo) as h:
                        n = dve.snap(passes, min_val=0, max_val=PASSES * B * CH)
                        for P in range(PAIRS + 4):
                            if 2 <= P < PAIRS + 2:
                                Q = P - 2
                                dve.wait_ge(S("sumx"), n * PAIRS + Q + 1)
                                if Q >= 3:
                                    dve.wait_ge(S("sumyd"), n * PAIRS + Q - 2)
                                v.tensor_tensor(prod[:, Q % 3], pair_of(3 + 2 * (Q % 2)), hY[:, Q % 2], ALU.mult) \
                                    .then_inc(S("prod"), 1)
                            if P < PAIRS:
                                dve.wait_ge(S("absx"), n * PAIRS + (P + 1 + BASE))
                                if P >= 2:
                                    dve.wait_ge(S("prod"), n * PAIRS + P - 1)
                                for s in (0, 1):
                                    half = slice(64 * s, 64 * s + 64)
                                    v.tensor_scalar(hX[P % 2][half, s, :], aX[half, P % 2, :], 1.0, 1.0, ALU.min,
                                                    ALU.subtract)
                                dve.wait_ge(S("abs"), n * PAIRS + (P + 1 + BASE))
                                v.tensor_scalar(hY[:, P % 2], aY[:, P % 2], 1.0, 1.0, ALU.min, ALU.subtract) \
                                    .then_inc(S("hat"), 1)
                            if P - 3 in last_pair:
                                f = last_pair.index(P - 3)
                                dve.wait_ge(S("sumyd"), n * PAIRS + last_pair[f] + 1)
                                v.tensor_tensor(T2[:, f, :], bank(7), maskE[:, f, :], ALU.mult) \
                                    .then_inc(S("T2"), 1)
                        dve.wait_ge(S("y3_ps"), BASE + n + 1)
                        dve.wait_ge(S("y3i"), c1)
                        dve.wait_ge(S("y3"), BASE + n)
                        v.tensor_tensor(y3c[:], bank(0, C), y3c[:], ALU.add).then_inc(S("y3"), 1)
                        dve.reg_add(passes, passes, 1)
                    ln("l2", "l2g", c1)
                    dve.wait_ge(S("l2_n"), c1)
                    v.tensor_scalar(ln_out[:], xn[:], k("l2b", C), None, ALU.add).then_inc(S("m3_in"), 1)
                    dwnorm(dve.snap(i * (CH + 1) + (t + 2)))
                    dve.wait_ge(S("m3_out"), c1)
                    v.scalar_tensor_tensor(y4c[:], bank(4, C), k("f2b", C), y3c[:], ALU.add, ALU.add) \
                        .then_inc(S("y4"), 1)
                    dve.wait_ge(S("oN_ps"), c1)
                    dve.wait_ge(S("stored"), BASE * 16 + 16 * c)
                    v.tensor_copy(oN[:].rearrange("p t c -> p (t c)"), bank(0, TP, TPC * C)).then_inc(S("oN"), 1)

        @block.gpsimd
        def _(pool):
            pool.sem_inc(S("xinP"), BASE)
            g = nc.gpsimd
            g.memset(h1p[:], 0.0).then_inc(S("cleared"), 1)
            g.memset(xinP[:], 0.0).then_inc(S("cleared"), 1)
            g.memset(imgF[:], 0.0).then_inc(S("cleared"), 1)
            g.memset(attnT[:], 0.0).then_inc(S("cleared"), 1)
            g.memset(y0T[:, T:], 0.0).then_inc(S("cleared"), 1)
            g.memset(imgW[:], 0.0).then_inc(S("cleared"), 1)
            pool.wait_ge(S("cleared"), 6)
            pool.wait_ge(S("consts"), 32)
            passes = pool.alloc_register("passes_pool")
            pool.reg_mov(passes, 0)
            with pool.Fori(0, B) as i:
                with pool.Fori(0, CH) as t:
                    c = i * CH + t
                    c1 = c + 1
                    pool.wait_ge(S("k"), i * (CH + 1) + (t + 1))
                    for w in range(NW):
                        if w >= 2:
                            pool.wait_ge(S("score_ps"), c * NW + (w - 1))
                        g.tensor_tensor(kexp[w % 2].rearrange("p (h m) -> p h m", h=HEADS),
                                        bc(kS[:, 64 * w:64 * w + 64].rearrange("p (o m) -> p o m", o=1), (128, 8, 64)),
                                        bc(k("hmask").rearrange("p (h o) -> p h o", o=1), (128, 8, 64)),
                                        ALU.mult).then_inc(S("kexp"), 1)
                    wait_apart(pool, S("y2"), c1)
                    g.tensor_copy(y2T[:, bass.ds(t * N, N)], y2c).then_inc(S("y2T"), 1)
                    wait_apart(pool, S("xin"), c1)
                    g.tensor_copy(xinP[:, bass.ds(t * ROWS + 1, ROWS), 1:1 + HW],
                                  xin.rearrange("p (r c) -> p r c", c=HW)).then_inc(S("xinP"), 1)
                with pool.Fori(0, CH) as t:
                    c = i * CH + t
                    c1 = c + 1
                    wait_apart(pool, S("npass"), c1)
                    todo = pool.value_load(npass[0:1, 0:1], min_val=1, max_val=PASSES)
                    with pool.Fori(0, todo) as h:
                        n = pool.snap(passes, min_val=0, max_val=PASSES * B * CH)
                        wait_apart(pool, S("img"), BASE + i * CH + CH)
                        wait_apart(pool, S("y3_ps"), BASE + n)
                        g.tensor_copy(ycol[:], K[:, bass.ds(COL["yneg"][0] + t + h * (WROWS // 8), 1)])
                        g.tensor_copy(imgW[:], imgF[:, :, bass.ds(t * ROWS + h * WROWS, WROWS)]).then_inc(S("imgW"), 1)
                        pool.reg_add(passes, passes, 1)


def kernel(**inp):
    import numpy as np
    import ml_dtypes
    import concourse.bacc as bacc
    from concourse import mybir as mb
    from concourse.bass_utils import run_bass_kernel_spmd as run

    f = np.float32
    a = {n: np.asarray(v) for n, v in inp.items()}
    W = np.zeros((128, NCOL), f)

    def put(name, val, row0=0, lo=0):
        at, size = COL[name]
        val = val.reshape(val.shape[0], -1)
        W[row0:row0 + val.shape[0], at + lo:at + lo + val.shape[1]] = val

    col = lambda v: v.reshape(-1, 1)
    put("ident", np.eye(128, dtype=f))
    put("w1", a["L1_conv_w1"][0, 0])
    w2 = np.zeros((128, 9, 128), f)
    for g in range(32):
        w2[4 * g:4 * g + 4, :, 4 * g:4 * g + 4] = \
            a["L1_conv_w2"].reshape(9, 4, 128)[:, :, 4 * g:4 * g + 4].transpose(1, 0, 2)
    put("w2", w2)
    put("w3", a["L1_conv_w3"][0, 0])
    for j, n in enumerate(["b1", "g1", "be1", "m1", "v1", "b2", "g2", "be2", "m2", "v2"]):
        put("bn", col(a["L1_conv_" + n]), 0, j)
    put("b3", col(a["L1_conv_b3"]))
    put("center", np.eye(64, dtype=f) - f(1 / 64))
    put("mean", np.full((64, 64), 1 / 64, f))
    for n, m in [("n1w", "norm1_w"), ("n1b", "norm1_b"), ("n2w", "norm2_w"), ("n2b", "norm2_b"),
                 ("projb", "proj_b"), ("fc2b", "fc2_b")]:
        put(n, col(a["L2_conv_" + m]))
    qkv = a["L2_conv_qkv_w"]
    for br in range(2):
        for j, n in enumerate(["wq", "wk", "wv"]):
            put(n, qkv[64 * j:64 * j + 64].T, 64 * br, 64 * br)
        put("bq", col(a["L2_conv_qkv_b"][0:64]), 64 * br)
        put("bv", np.broadcast_to(a["L2_conv_qkv_b"][128:192], (64, 64)), 64 * br)
    tt = np.arange(64)[:, None]
    kr, ki = np.arange(33)[None], np.arange(1, 32)[None]
    ang = lambda kk: 2 * np.pi * ((kk * tt) % 64) / 64
    put("dft", np.concatenate([np.cos(ang(kr)), -np.sin(ang(ki))], 1).astype(f) / f(8))
    wr = np.where((kr == 0) | (kr == 32), 1.0, 2.0)
    put("idft", np.eye(64, dtype=f))
    put("idft", (np.concatenate([wr * np.cos(ang(kr)), -2 * np.sin(ang(ki))], 1) / 8).T.astype(f), 64)
    ch = np.arange(8)
    co = np.stack(np.meshgrid(ch, ch, indexing="ij")).reshape(2, -1)
    rel = (co[0][:, None] - co[0][None] + 7) * 15 + co[1][:, None] - co[1][None] + 7
    put("rel", a["L2_conv_rpb_table"][rel].transpose(0, 2, 1))
    put("hmask", np.kron(np.ones((2, 1), f), np.kron(np.eye(8, dtype=f), np.ones((8, 1), f))))
    put("vmask", np.kron(np.ones((1, 8), f), np.kron(np.eye(2, dtype=f), np.ones((64, 8), f))))
    put("floor", np.full((64, 1), -3e38, f))
    put("zeros2", np.full((64, 1), 2, f), 64)
    put("proj", a["L2_conv_proj_w"].T)
    put("fc1", a["L2_conv_fc1_w"].T)
    put("fc1b", a["L2_conv_fc1_b"].reshape(2, 128).T)
    put("fc2", a["L2_conv_fc2_w"].T.reshape(2, 128, 64).transpose(1, 0, 2))
    for n, m in [("l1g", "ln1_g"), ("l1b", "ln1_b"), ("dwb", "dw_b"), ("dwg", "dwln_g"), ("dwbeta", "dwln_b"),
                 ("outb", "outproj_b"), ("l2g", "ln2_g"), ("l2b", "ln2_b"), ("f2b", "fc2_b")]:
        put(n, col(a["L3_conv_" + m]))
    dw = np.zeros((64, 9, 128), f)
    dw[np.arange(64), :, np.arange(64)] = a["L3_conv_dw_w"].reshape(9, 64).T
    put("dw", dw)
    off = np.zeros((XR, UNITS * 2), f)
    off[0:64] = a["L3_conv_off_w"]
    off[64, 0::2] = 1
    off[65, 1::2] = 1
    off[66] = a["L3_conv_off_b"]
    pts = np.arange(UNITS) % KP
    off[67, 0::2] = pts // 3 - 1
    off[67, 1::2] = pts % 3 - 1
    put("off", np.broadcast_to(off.reshape(XR, OBLK, 1, 32), (XR, OBLK, 3, 32)))
    mk, raw = np.zeros((XR, UNITS), f), np.zeros((XR, UNITS), f)
    raw[0:64] = a["L3_conv_off_w"][:, 1::2]
    raw[66] = a["L3_conv_off_b"][1::2]
    mk[0:64] = a["L3_conv_mask_w"]
    mk[66] = a["L3_conv_mask_b"]
    put("mask", np.concatenate([mk, raw], 1))
    put("inw", a["L3_conv_inproj_w"])
    put("inb", np.broadcast_to(a["L3_conv_inproj_b"], (128, 64)))
    ow = np.zeros((128, FBLK, 64), f)
    for u in range(UNITS):
        fb, q, kk = u // 32, u % 4, (u % 32) // 4
        ow[32 * q + 4 * kk:32 * q + 4 * kk + 4, fb] = a["L3_conv_outproj_w"][4 * (u // KP):4 * (u // KP) + 4]
    put("outw", ow)
    put("f1", a["L3_conv_fc1_w"])
    put("f1b", a["L3_conv_fc1_b"].reshape(2, 128).T)
    put("f2", a["L3_conv_fc2_w"].reshape(2, 128, 64).transpose(1, 0, 2))
    for n, e in EPS.items():
        put(n, np.full((128, 1), e, f))
    p = np.arange(128)
    sy = np.zeros((128, 60), f)
    sy[p, 28 + p // WROWS] = 1
    put("sumy", sy)
    put("xneg", -(p % 64).astype(f)[:, None])
    put("yneg", -((8 * np.arange(CH + WROWS // 8)[None] + (p % WROWS)[:, None] - LEAD) % 64).astype(f))
    coords = np.ones((4, T + N), f)
    coords[0] = np.arange(T + N) % HW
    coords[1] = np.arange(T + N) // HW
    sel = np.zeros((4, 32, 8, 3, 128), f)
    for j in range(8):
        sel[0:3, 4 * j, j, 0, 0:64] = 1
        sel[0:3, 4 * j + 2, j, 0, 64:128] = 1
        sel[0:3, 4 * j + 1, j, 1] = 1
        sel[0:3, 4 * j + 3, j, 2] = 1
    sel = sel.reshape(128, -1).astype(ml_dtypes.bfloat16)

    arrays = {"x_in": np.ascontiguousarray(a["x"].reshape(B, T, C)), "consts_in": W, "coords_in": coords,
              "sel_in": sel}
    nc = bacc.Bacc("TRN2", target_bir_lowering=False, num_devices=1)
    args = [nc.dram_tensor(n, v.shape, mb.dt.from_np(v.dtype), kind="ExternalInput").ap() for n, v in arrays.items()]
    o = nc.dram_tensor("out_0", (B, T, C), mb.dt.float32, kind="ExternalOutput").ap()
    build(nc, *args, o)
    r = run(nc, [arrays], core_ids=[0])
    return r.results[0]["out_0"].reshape(B, HW, HW, C)
```
